# Optimizing a Trainium2 kernel written in Bass

```python
import numpy as np
import jax
import jax.numpy as jnp

def _softmax(x, axis=-1):
    return jax.nn.softmax(x, axis=axis)
def _gelu(x):
    return jax.nn.gelu(x, approximate=True)
def _silu(x):
    return jax.nn.silu(x)
def _sigmoid(x):
    return jax.nn.sigmoid(x)
def _layernorm(x, axis=-1, eps=1e-5):
    m = jnp.mean(x, axis=axis, keepdims=True)
    v = jnp.var(x, axis=axis, keepdims=True)
    return (x - m) / jnp.sqrt(v + eps)
def _scatter_add(tgt, idx, src, axis=0):
    return tgt.at[idx].add(src)
def _segment_sum(src, seg, n):
    return jax.ops.segment_sum(src, seg, n)

kernel_name = 'mk_conv_preact_d2_conv_nchw96_a0aab5'

def setup_inputs(seed: int = 0):
    np.random.seed(seed)
    _w = jnp.asarray
    def _rec_inputs():
        import jax
        import jax.numpy as jnp
        _gk = jax.random.key(seed)
        x = -4.65e-05 + 0.9999 * jax.random.normal(jax.random.fold_in(_gk, 1), (8, 96, 256, 256), jnp.float32)
        return x
    x = _rec_inputs()
    def _L0_conv_setup():
        import jax, jax.numpy as jnp
        import numpy as np
        DIM = 96
        HEADS = 6
        EPS = 1e-12

        def _conv(x, w, padding, groups=1):
            return jax.lax.conv_general_dilated(x, w, window_strides=(1, 1), padding=padding, dimension_numbers=('NCHW', 'OIHW', 'NCHW'), feature_group_count=groups)
        key = jax.random.key(seed)
        k0, k1, k2, k3 = jax.random.split(key, 4)
        B, C, H, W = (8, DIM, 256, 256)
        x = jax.random.normal(k0, (B, C, H, W), dtype=jnp.float32)
        qkv_w = jax.random.normal(k1, (3 * C, C, 1, 1), dtype=jnp.float32) * 0.05
        qkv_dw_w = jax.random.normal(k2, (3 * C, 1, 3, 3), dtype=jnp.float32) * 0.05
        proj_w = jax.random.normal(k3, (C, C, 1, 1), dtype=jnp.float32) * 0.05
        return {'x': x, 'qkv_w': qkv_w, 'qkv_dw_w': qkv_dw_w, 'proj_w': proj_w}
    _L0_conv_all = _L0_conv_setup()
    _L0_conv_in = {k: v for k, v in _L0_conv_all.items() if k in ('qkv_w', 'qkv_dw_w', 'proj_w', )}
    del _L0_conv_all

    def _L1_conv_setup():
        import jax, jax.numpy as jnp
        import numpy as np
        DIM = 96
        K = 3
        STRIDE = 1
        PAD = 1
        RED = 4
        BN_EPS = 1e-05

        def _dynamic_weight(x, w1, gamma, beta, running_mean, running_var, w2, b2):
            pooled = jnp.mean(x, axis=(2, 3))
            h1 = pooled @ w1.T
            h1 = (h1 - running_mean) * jax.lax.rsqrt(running_var + BN_EPS) * gamma + beta
            h1 = jax.nn.sigmoid(h1)
            wdyn = h1 @ w2.T + b2
            return wdyn.reshape(x.shape[0], DIM, K, K)

        def _per_sample_depthwise(x, weight, bias):

            def one(xi, wi):
                out = jax.lax.conv_general_dilated(xi[None], wi[:, None], window_strides=(STRIDE, STRIDE), padding=[(PAD, PAD), (PAD, PAD)], dimension_numbers=('NCHW', 'OIHW', 'NCHW'), feature_group_count=DIM)
                return out[0]
            y = jax.vmap(one)(x, weight)
            return y + bias[None, :, None, None]
        key = jax.random.key(seed)
        ks = jax.random.split(key, 8)
        b, c, h, w = (32, DIM, 128, 128)
        cr = DIM // RED
        return {'x': jax.random.normal(ks[0], (b, c, h, w), jnp.float32), 'w1': jax.random.normal(ks[1], (cr, c), jnp.float32) * 0.1, 'gamma': jnp.ones((cr,), jnp.float32), 'beta': jnp.zeros((cr,), jnp.float32), 'running_mean': jax.random.normal(ks[2], (cr,), jnp.float32) * 0.1, 'running_var': jax.random.uniform(ks[3], (cr,), jnp.float32, 0.5, 1.5), 'w2': jax.random.normal(ks[4], (DIM * K * K, cr), jnp.float32) * 0.1, 'b2': jax.random.normal(ks[5], (DIM * K * K,), jnp.float32) * 0.1, 'bias': jnp.zeros((DIM,), jnp.float32)}
    _L1_conv_all = _L1_conv_setup()
    _L1_conv_in = {k: v for k, v in _L1_conv_all.items() if k in ('w1', 'gamma', 'beta', 'running_mean', 'running_var', 'w2', 'b2', 'bias', )}
    del _L1_conv_all

    return {
        "x": x,
        "L0_conv_qkv_w": _L0_conv_in["qkv_w"],
        "L0_conv_qkv_dw_w": _L0_conv_in["qkv_dw_w"],
        "L0_conv_proj_w": _L0_conv_in["proj_w"],
        "L1_conv_w1": _L1_conv_in["w1"],
        "L1_conv_gamma": _L1_conv_in["gamma"],
        "L1_conv_beta": _L1_conv_in["beta"],
        "L1_conv_running_mean": _L1_conv_in["running_mean"],
        "L1_conv_running_var": _L1_conv_in["running_var"],
        "L1_conv_w2": _L1_conv_in["w2"],
        "L1_conv_b2": _L1_conv_in["b2"],
        "L1_conv_bias": _L1_conv_in["bias"],
    }

def reference(x, L0_conv_qkv_w, L0_conv_qkv_dw_w, L0_conv_proj_w, L1_conv_w1, L1_conv_gamma, L1_conv_beta, L1_conv_running_mean, L1_conv_running_var, L1_conv_w2, L1_conv_b2, L1_conv_bias):
    import jax
    import jax.numpy as jnp
    def _L0_conv_ref(x, qkv_w, qkv_dw_w, proj_w):
        import jax, jax.numpy as jnp
        import numpy as np
        DIM = 96
        HEADS = 6
        EPS = 1e-12

        def _conv(x, w, padding, groups=1):
            return jax.lax.conv_general_dilated(x, w, window_strides=(1, 1), padding=padding, dimension_numbers=('NCHW', 'OIHW', 'NCHW'), feature_group_count=groups)
        B, C, H, W = x.shape
        heads = HEADS
        hd = C // heads
        scale = hd ** (-0.5)
        qkv = _conv(x, qkv_w, 'VALID')
        qkv = _conv(qkv, qkv_dw_w, 'SAME', groups=3 * C)
        q, k, v = jnp.split(qkv, 3, axis=1)

        def rs(t):
            return t.reshape(B, heads, hd, H * W)
        q, k, v = (rs(q), rs(k), rs(v))
        q = q / jnp.maximum(jnp.linalg.norm(q, axis=-1, keepdims=True), EPS)
        k = k / jnp.maximum(jnp.linalg.norm(k, axis=-1, keepdims=True), EPS)
        attn = jnp.einsum('bhcn,bhdn->bhcd', q, k) * scale
        attn = jax.nn.softmax(attn, axis=-1)
        out = jnp.einsum('bhcd,bhdn->bhcn', attn, v).reshape(B, C, H, W)
        return _conv(out, proj_w, 'VALID')

    def _L1_conv_ref(x, w1, gamma, beta, running_mean, running_var, w2, b2, bias):
        import jax, jax.numpy as jnp
        import numpy as np
        DIM = 96
        K = 3
        STRIDE = 1
        PAD = 1
        RED = 4
        BN_EPS = 1e-05

        def _dynamic_weight(x, w1, gamma, beta, running_mean, running_var, w2, b2):
            pooled = jnp.mean(x, axis=(2, 3))
            h1 = pooled @ w1.T
            h1 = (h1 - running_mean) * jax.lax.rsqrt(running_var + BN_EPS) * gamma + beta
            h1 = jax.nn.sigmoid(h1)
            wdyn = h1 @ w2.T + b2
            return wdyn.reshape(x.shape[0], DIM, K, K)

        def _per_sample_depthwise(x, weight, bias):

            def one(xi, wi):
                out = jax.lax.conv_general_dilated(xi[None], wi[:, None], window_strides=(STRIDE, STRIDE), padding=[(PAD, PAD), (PAD, PAD)], dimension_numbers=('NCHW', 'OIHW', 'NCHW'), feature_group_count=DIM)
                return out[0]
            y = jax.vmap(one)(x, weight)
            return y + bias[None, :, None, None]
        weight = _dynamic_weight(x, w1, gamma, beta, running_mean, running_var, w2, b2)
        return _per_sample_depthwise(x, weight, bias)

    def _gn(v, G=32, eps=1e-5):
        B_, C_, H_, W_ = v.shape
        g = v.reshape(B_, G, C_ // G, H_, W_)
        m = jnp.mean(g, axis=(2, 3, 4), keepdims=True)
        s = jnp.var(g, axis=(2, 3, 4), keepdims=True)
        return ((g - m) / jnp.sqrt(s + eps)).reshape(v.shape)

    def _ln_c(v, eps=1e-6):
        m = jnp.mean(v, axis=1, keepdims=True)
        s = jnp.var(v, axis=1, keepdims=True)
        return (v - m) / jnp.sqrt(s + eps)

    def _ln_t(v, eps=1e-5):
        m = jnp.mean(v, axis=-1, keepdims=True)
        s = jnp.var(v, axis=-1, keepdims=True)
        return (v - m) / jnp.sqrt(s + eps)

    def _to_tokens(v):
        B_, C_, H_, W_ = v.shape
        return v.reshape(B_, C_, H_ * W_).transpose(0, 2, 1)
    def _from_tokens(t, like):
        B_, C_, H_, W_ = like.shape
        return t.transpose(0, 2, 1).reshape(B_, C_, H_, W_)

    x = x + _L0_conv_ref(_gn(x), L0_conv_qkv_w, L0_conv_qkv_dw_w, L0_conv_proj_w)
    x = x + _L1_conv_ref(_gn(x), L1_conv_w1, L1_conv_gamma, L1_conv_beta, L1_conv_running_mean, L1_conv_running_var, L1_conv_w2, L1_conv_b2, L1_conv_bias)
    return x


_drawn_inputs = setup_inputs


def setup_inputs(seed=0):
    import zlib

    import numpy as np

    out = dict(_drawn_inputs(seed))
    spreads = {'L1_conv_gamma': (1.0, 0.6), 'L1_conv_beta': (0.0, 0.515), 'L1_conv_bias': (0.0, 0.1)}
    factors = {'L0_conv_qkv_w': 6.448,
     'L0_conv_qkv_dw_w': 6.269,
     'L0_conv_proj_w': 6.134,
     'L1_conv_w1': 200.0,
     'L1_conv_running_var': 200.0,
     'L1_conv_running_mean': 23.289}
    for name, (base, spread) in spreads.items():
        noise = np.random.default_rng([zlib.crc32(name.encode()), seed]).standard_normal(out[name].shape)
        drawn = base * np.exp(spread * noise) if base else spread * noise
        out[name] = jnp.asarray(drawn.astype(out[name].dtype))
    for name, factor in factors.items():
        out[name] = (out[name] * factor).astype(out[name].dtype)
    return out
```

```python
from contextlib import ExitStack

import numpy as np

import concourse.bass as bass
from concourse import mybir

B, C, H, W = 8, 96, 256, 256
HEADS = 6
HD = C // HEADS
GN_GROUPS = 32
CPG = C // GN_GROUPS
RED = 24
K1 = C + 1
QK = 2 * C
GN_EPS = 1e-5
BN_EPS = 1e-5
NORM_EPS = 1e-12
TAPS = 9

WP = W + 4
CH = 16
XROWS = CH + 2
NIT = H // (2 * CH)
RING = 2 * CH
LAG = 6
LAGS = [(0, dy) for dy in range(3)] + [(dx, dy) for dx in (1, 2) for dy in range(-2, 3)]
NL = len(LAGS)
LAG_W = 5 * K1

CG = 4
SR, SO = 32, 30
NG = C // CG
NS = -(-H // SO)
LAST = H - SO * (NS - 1)
HP = SO * (NS - 1) + SR
XW = W + 2
NV = TAPS + 2
EDGE_N = [(i, n) for i in range(2) for n in range(3)] + [(i, n) for i in (2, 3) for n in range(2)]
EP = (W + 2) // 3

COLS = {}
_at = 0
for _name, _n in (("ident", 128), ("avg_sum", C), ("avg_mean", C), ("spread_in", CG * SR),
                  ("spread_out", CG * SO), ("group_of", NG), ("off_head", C),
                  ("band", 3 * CG * SO), ("strip_rows", 3), ("zero", K1)):
    COLS[_name] = (_at, _at + _n)
    _at += _n
NCONST = _at


def constants():
    t = np.zeros((128, NCONST), np.float32)

    def part(name):
        a, b = COLS[name]
        return t[:, a:b]

    part("ident")[:] = np.eye(128)
    c = np.arange(C)
    same = c[:, None] // CPG == c[None] // CPG
    part("avg_sum")[:C] = same / (CPG * H * W)
    part("avg_mean")[:C] = same / CPG
    part("spread_in")[:C] = c[:, None] % CG == np.arange(CG * SR)[None] // SR
    part("spread_out")[:C] = c[:, None] % CG == np.arange(CG * SO)[None] // SO
    part("group_of")[:C] = c[:, None] // CG == np.arange(NG)[None]
    part("off_head")[:C] = np.where(c[:, None] // HD == c[None] // HD, 0.0, -1e30)
    p, m = np.arange(CG * SR)[:, None], np.arange(CG * SO)[None]
    for dy in range(3):
        part("band")[:, dy * CG * SO:(dy + 1) * CG * SO] = (p // SR == m // SO) & (p % SR == m % SO + dy)
    rows = part("strip_rows")
    rows[:, 0] = p[:, 0] % SR > 0
    rows[:, 1] = 1
    rows[:, 2] = p[:, 0] % SR <= LAST
    return t


PE_STEPS = (["means0", "folded", "folded_v"] + [f"lag_w{j}" for j in range(7)] + [f"lag_qk{d}" for d in range(NL)]
            + [f"ring{j}" for j in range(10)] + ["ring_qk", "dots_t", "logits", "attn_proj", "conv_a", "conv_b",
                                                "means1", "hidden", "dynamic", "spread", "spread_bias"])
DVE_STEPS = (["lags0", "squares0", "sums0", "sumsq0", "mean0", "meansq0", "var0", "vareps0", "rstd0", "fold_diag0",
              "fold0", "folded_qk", "ring_taps"]
             + [f"lag_dots{d}" for d in range(NL)]
             + ["dots", "dots_ring", "own", "own_sum", "norm_sq", "norm_inv", "norm_q", "dots_kq", "dots_k",
                "masked", "max", "max_neg", "sum_inv", "attn", "v_taps", "conv_0", "conv_4", "conv_5",
                "clear1", "channel1", "first1", "mean_sq1", "second1", "mean1", "meansq1", "var1", "vareps1", "rstd1", "pooled",
                "dyn_b2", "taps1", "taps1_res", "col_mean", "col_bias", "columns", "taps_spread", "strip_means"])
ACT_STEPS = (["lags1", "lags2", "std0", "folded_v"] + [f"lag_w{j}" for j in range(7)]
             + [f"ring{j}" for j in range(10)] + ["norm", "exp", "std1", "gate", "bias_spread"])


def at(steps, name):
    return steps.index(name) + 1


def build(nc, x, qkv_wT, dw_t, lag_t, dw_rep, dw_v, proj_wT, w1T, bn, w2T, b2, bias, const, out):
    f32 = mybir.dt.float32
    ALU = mybir.AluOpType
    ACT = mybir.ActivationFunctionType
    AX = mybir.AxisListType.X
    x1_dram = nc.dram_tensor("x1", [C, HP, W], f32, kind="Internal").ap()
    NPE, NDVE, NACT = len(PE_STEPS), len(DVE_STEPS), len(ACT_STEPS)

    with ExitStack() as ctx:
        def sb(name, shape):
            return ctx.enter_context(nc.sbuf_tensor(name, shape, f32))

        def sem(name):
            return ctx.enter_context(nc.semaphore(name))

        xc = [sb(f"x_chunk_{n}", [K1, XROWS, WP]) for n in "ab"]
        xt = sb("x_transposed", [128, RING, 4, K1])
        stage = [sb(f"stage_{n}", [128, CH * W]) for n in "ab"]
        x1_out = [s[0:C, :].rearrange("p (r w) -> p r w", w=W) for s in stage]
        ys = [s[0:CG * SO, 0:NS * W].rearrange("p (s w) -> p s w", w=W) for s in stage]
        xs = [sb(f"x1_strips_{n}", [CG * SR, NS, XW]) for n in "ab"]
        bands = [sb(f"bands_{n}", [CG * SR, 3, CG * SO]) for n in "ab"]
        ct = sb("constants", [128, NCONST])
        w_qkvT = sb("w_qkvT", [C, 3 * C])
        w_projT = sb("w_projT", [C, C])
        w_1T = sb("w_1T", [C, RED])
        w_2T = sb("w_2T", [RED, TAPS, C])
        b_2 = sb("b_2", [C, TAPS])
        b_out = sb("b_out", [C, 1])
        v_dw = sb("v_dw", [C, TAPS])
        bn_in = sb("bn_in", [RED, 4])
        bn_sb = sb("bn_scale_shift", [RED, 4])
        taps_qk = sb("taps_qk", [TAPS, QK])
        taps_lag = xt[0:TAPS, :, :, :].rearrange("p r s c -> p (r s c)")[:, 0:NL * QK].rearrange("p (d c) -> p d c", d=NL)
        lag_coef = sb("lag_coef", [C, NL, 2 * QK])
        edge_rows = sb("edge_rows", [K1, 2, WP])
        edge_cols = sb("edge_cols", [K1, 2, H + 2])
        lags = sb("lags", [K1, 3, LAG_W])
        conv_w = sb("conv_w", [K1, TAPS, C])
        x1_stats = sb("x1_stats", [C, H // 2, 6])
        flat = xt[:, :, :, :].rearrange("p r s c -> p (r s c)")

        def shared(first, parts, n):
            return flat[0:parts, first:first + n]

        lagw = shared(0, K1, NL * QK).rearrange("p (d a) -> p d a", d=NL)
        dots_all = shared(NL * QK, C, NL * 2 * QK).rearrange("p (d a) -> p d a", d=NL)
        ring_w = shared(3 * NL * QK, K1, TAPS * QK).rearrange("p (t a) -> p t a", t=TAPS)
        v_taps = shared(3 * NL * QK + TAPS * QK, C, TAPS * C).rearrange("p (t a) -> p t a", t=TAPS)
        assert 3 * NL * QK + TAPS * (QK + C) <= RING * 4 * K1
        dw_all = sb("dw_all", [K1, TAPS, QK])
        sq0 = sb("sq0", [C, C])
        st0 = sb("st0", [C, 2])
        gm0 = sb("gm0", [C, 6])
        fold = sb("fold", [C, K1])
        w_fold = sb("w_fold", [K1, QK])
        v_fold = sb("v_fold", [C, K1])
        ring_sb = sb("ring_sb", [128, 2, QK])
        dots = sb("dots", [C, 2 * QK])
        dots2 = sb("dots2", [C, 2 * QK])
        own = sb("own", [C, 2, C])
        nrm = sb("nrm", [C, 10])
        att = sb("att", [C, 5, C])
        mv1 = sb("mv1", [C, 2])
        st1 = sb("st1", [C, 2])
        gm1 = sb("gm1", [C, 8])
        hid = sb("hid", [RED, 1])
        dyn = sb("dyn", [C, TAPS])
        vec1 = sb("vec1", [C, NV])
        cols1 = sb("cols1", [C, NG, NV])
        taps1 = sb("taps1", [CG * SR, NG, NV])
        bias1 = sb("bias1", [CG * SO, NG])
        spare = sb("spare", [CG * SO, 2])
        bias_g = sb("bias_g", [CG * SO, 2])
        means1 = sb("means1", [CG * SR, NG, 3])

        def const_(name, parts):
            a, b = COLS[name]
            return ct[0:parts, a:b]

        def ps(name):
            return ctx.enter_context(nc.psum_tensor(name, [128, 512], f32))

        acc = [ps(f"lag_acc{i}") for i in range(3)]
        bank = [ps(f"bank{i}") for i in range(5)]

        setup_loaded = sem("setup_loaded")
        setup_zeros = sem("setup_zeros")
        setup_pads = sem("setup_pads")
        setup_pe = sem("setup_pe")
        setup_dve = sem("setup_dve")
        setup_act = sem("setup_act")
        x_loaded = [sem(f"x_loaded_{n}") for n in "ab"]
        edge_rows_loaded = sem("edge_rows_loaded")
        edges_taken = [sem(f"edges_taken_{n}") for n in "ab"]
        row_turned = sem("row_turned")
        row_kept = sem("row_kept")
        lags_summed = sem("lags_summed")
        pe_step, dve_step, act_step = sem("pe_step"), sem("dve_step"), sem("act_step")
        x1_ready = sem("x1_ready")
        x1_copied = sem("x1_copied")
        x1_counted = [sem(f"x1_counted_{n}") for n in "ab"]
        x1_stored = [sem(f"x1_stored_{n}") for n in "ab"]
        xs_loaded = [sem(f"xs_loaded_{n}") for n in "ab"]
        xs_centred = sem("xs_centred")
        band_step = sem("band_step")
        y_ready = sem("y_ready")
        y_copied = [sem(f"y_copied_{i}") for i in range(5)]
        bias_taken = sem("bias_taken")
        y_stored = [sem(f"y_stored_{n}") for n in "ab"]

        SETUP_DMAS = 12
        NZ = NIT * 2
        NGI = NG // 2
        PAIRS = H // 2
        YU = (NS + 1) // 2
        block = ctx.enter_context(nc.Block())

        @block.sync
        def _(sp):
            for dst, src in ((ct[:, :], const), (w_qkvT[:, :], qkv_wT), (w_projT[:, :], proj_wT), (w_1T[:, :], w1T),
                             (w_2T[:, :, :], w2T), (b_2[:, :], b2), (b_out[:, :], bias), (v_dw[:, :], dw_v),
                             (bn_in[:, :], bn), (taps_qk[:, :], dw_t), (taps_lag, lag_t),
                             (dw_all[:, :, :], dw_rep)):
                sp.dma_start(dst, src).then_inc(setup_loaded, 16)
            sp.wait_ge(setup_zeros, 1)
            sp.dma_start(x1_dram[:, 0:1, :], xc[0][0:C, 0:1, 0:W]).then_inc(setup_pads, 16)
            sp.dma_start(x1_dram[:, H + 1:HP, :], xc[0][0:C, 0:HP - H - 1, 0:W]).then_inc(setup_pads, 16)
            sp.wait_ge(setup_pads, 32)
            sp.wait_ge(setup_zeros, 9)
            with sp.Fori(0, B) as b:
                xb = x[bass.ds(b, 1), :, :, :].rearrange("b c h w -> (b c) h w")
                sp.wait_ge(x1_ready, b * PAIRS)
                for i in range(2):
                    sp.dma_start(xc[i][0:C, 0:CH, 2:2 + W], xb[:, i * CH:(i + 1) * CH, :]).then_inc(x_loaded[i], 16)
                for i in range(2):
                    sp.dma_start(edge_rows[0:C, i, 2:2 + W], xb[:, i * (H - 1), :]).then_inc(edge_rows_loaded, 16)
                with sp.Fori(1, NIT) as k:
                    for i in range(2):
                        sp.wait_ge(row_turned, b * H + k * RING + (i - 1) * CH)
                        sp.wait_ge(edges_taken[i], b * NIT + k)
                        sp.dma_start(xc[i][0:C, 0:CH, 2:2 + W], xb[:, bass.ds(k * 2 * CH + i * CH, CH), :]).then_inc(
                            x_loaded[i], 16)
                for i in range(2):
                    sp.wait_ge(row_turned, b * H + H + (i - 1) * CH)
                    sp.wait_ge(edges_taken[i], b * NIT + NIT)
                    first = 1 - i
                    sp.dma_start(xc[i][0:C, first:XROWS, 2:2 + W],
                                 xb[:, i * CH - 1 + first:i * CH - 1 + XROWS, :]).then_inc(x_loaded[i], 16)
                with sp.Fori(1, NIT - 1) as k:
                    for i in range(2):
                        sp.wait_ge(x1_ready, b * PAIRS + k * CH + (i - 1) * CH // 2)
                        sp.dma_start(xc[i][0:C, :, 2:2 + W],
                                     xb[:, bass.ds(k * 2 * CH + i * CH - 1, XROWS), :]).then_inc(x_loaded[i], 16)
                for i in range(2):
                    sp.wait_ge(x1_ready, b * PAIRS + PAIRS - CH + (i - 1) * CH // 2)
                    n = XROWS - i
                    r0 = H - 2 * CH + i * CH - 1
                    sp.dma_start(xc[i][0:C, 0:n, 2:2 + W], xb[:, r0:r0 + n, :]).then_inc(x_loaded[i], 16)
                for i in range(2):
                    sp.wait_ge(x1_stored[i], (b + 1) * 16 * NIT)
                def load_strips(g, i):
                    for c in range(CG):
                        src = bass.AP(x1_dram.tensor, g * (2 * CG * HP * W) + (i * CG + c) * HP * W,
                                      [[W, SR], [SO * W, NS], [1, W]])
                        sp.dma_start(xs[i][c * SR:(c + 1) * SR, :, 1:1 + W], src).then_inc(xs_loaded[i], 16)

                sp.wait_ge(y_ready, b * YU * NG)
                for i in range(2):
                    load_strips(0, i)
                with sp.Fori(1, NGI) as g:
                    for i in range(2):
                        sp.wait_ge(y_ready, b * YU * NG + (g * 2 + i - 1) * YU)
                        load_strips(g, i)
            for i in range(2):
                sp.wait_ge(y_stored[i], 16 * 2 * CG * NGI * B)

        @block.gpsimd
        def _(pool):
            for i in range(2):
                nc.gpsimd.memset(xc[i][:, :, :], 0.0).then_inc(setup_zeros, 1)
                pool.wait_ge(setup_zeros, i + 1)
            pool.wait_ge(setup_pads, 32)
            n = 2
            for borders in (xs[0][:, :, :], xs[1][:, :, :], edge_cols[:, :, :], edge_rows[:, :, :]):
                nc.gpsimd.memset(borders, 0.0).then_inc(setup_zeros, 1)
                n += 1
                pool.wait_ge(setup_zeros, n)
            for ones in (xc[0][C:K1, :, 2:2 + W], xc[1][C:K1, :, 2:2 + W], edge_rows[C:K1, :, 2:2 + W]):
                nc.gpsimd.memset(ones, 1.0).then_inc(setup_zeros, 1)
                n += 1
                pool.wait_ge(setup_zeros, n)
            with pool.Fori(0, B) as b:
                with pool.Fori(0, NIT) as k:
                    pool.wait_ge(pe_step, b * NPE)
                    for i in range(2):
                        pool.wait_ge(x_loaded[i], b * 16 * NZ + k * 16 + 16)
                        at_row = 1 + k * 2 * CH + i * CH
                        nc.gpsimd.tensor_copy(edge_cols[:, 0, bass.ds(at_row, CH)], xc[i][:, 0:CH, 2])
                        ins = nc.gpsimd.tensor_copy(edge_cols[:, 1, bass.ds(at_row, CH)], xc[i][:, 0:CH, 1 + W])
                        ins.then_inc(edges_taken[i], 1)

        @block.tensor
        def _(pe):
            ident = const_("ident", K1)[:, 0:K1]
            ident_c = const_("ident", C)[:, 0:C]
            pe.wait_ge(setup_loaded, 16 * SETUP_DMAS)
            for d in range(NL):
                if d >= 5:
                    pe.wait_ge(setup_dve, d - 4)
                for half in range(2):
                    ins = nc.tensor.matmul(bank[d % 5][0:C, half * QK:(half + 1) * QK],
                                           taps_qk[:, half * C:(half + 1) * C], taps_lag[:, d, :],
                                           start=True, stop=True)
                ins.then_inc(setup_pe, 1)
            pe.wait_ge(setup_zeros, 9)
            pe.wait_ge(setup_dve, NL)

            def turn_row(b, k, r, first=False):
                if r % CH == 0:
                    pe.wait_ge(x_loaded[r // CH], b * 16 * NZ + k * 16 + 16)
                if not (first and r < 2):
                    pe.wait_ge(row_kept, b * H + k * RING + r - 1)
                for s in range(4):
                    ins = nc.tensor.transpose(bank[r % 2][:, s * K1:(s + 1) * K1],
                                              xc[r // CH][:, r % CH, 2 + s:2 + s + W - 1:2], ident)
                ins.then_inc(row_turned, 1)

            def lag_row(r, lo, hi):
                for s in range(2):
                    for dx in range(3):
                        a, e = (max(lo, 0), hi) if dx == 0 else (lo, hi)
                        base = 0 if dx == 0 else -2
                        while a <= e:
                            slot = (r + a) % RING
                            n = min(e - a + 1, RING - slot)
                            ins = nc.tensor.matmul(
                                acc[dx][0:K1, (a - base) * K1:(a - base + n) * K1],
                                xt[:, r % RING, s, :], xt[:, slot:slot + n, s + dx, :],
                                start=False, stop=False, skip_group_check=True)
                            a += n
                return ins

            with pe.Fori(0, B) as b:
                for j in range(5):
                    pe.wait_ge(y_copied[j], b * NG)
                for dx in range(3):
                    n = (3 if dx == 0 else 5) * K1
                    nc.tensor.matmul(acc[dx][0:K1, 0:n], const_("zero", 128),
                                     ct[:, 0:n], start=True, stop=False, skip_group_check=True)
                for r in range(RING):
                    turn_row(b, 0, r, first=True)
                    if r >= LAG:
                        q = r - LAG
                        pe.wait_ge(row_kept, b * H + q + 3)
                        lag_row(q, -min(q, 2), 2)
                with pe.Fori(1, NIT) as k:
                    for r in range(RING):
                        turn_row(b, k, r)
                        pe.wait_ge(row_kept, b * H + k * RING + r - LAG + 3)
                        lag_row(r + RING - LAG, -2, 2)
                for q in range(H - LAG, H):
                    pe.wait_ge(row_kept, b * H + min(q + 3, H))
                    ins = lag_row(q, -2, min(2, H - 1 - q))
                ins.then_inc(lags_summed, 1)

                def step(ins):
                    ins.then_inc(pe_step, 1)

                def dve(name):
                    pe.wait_ge(dve_step, b * NDVE + at(DVE_STEPS, name))

                def act(name):
                    pe.wait_ge(act_step, b * NACT + at(ACT_STEPS, name))

                small = bank[4]
                dve("sumsq0")
                step(nc.tensor.matmul(small[0:C, 0:2], const_("avg_sum", C), st0[:, :], start=True, stop=True))
                dve("fold0")
                step(nc.tensor.matmul(bank[2][0:K1, 0:QK], fold[:, :], w_qkvT[:, 0:QK], start=True, stop=True))
                step(nc.tensor.matmul(bank[3][0:C, 0:K1], w_qkvT[:, QK:3 * C], fold[:, :], start=True, stop=True))
                dve("folded_qk")
                act("lags2")
                for j in range(7):
                    if j >= 2:
                        act(f"lag_w{j - 2}")
                    for d in range(2 * j, min(2 * j + 2, NL)):
                        dx, i = (0, d) if d < 3 else (1 + (d - 3) // 5, (d - 3) % 5)
                        ins = nc.tensor.matmul(bank[j % 2][0:K1, (d % 2) * QK:(d % 2 + 1) * QK],
                                               lags[:, dx, i * K1:(i + 1) * K1], w_fold[:, :], start=True, stop=True)
                    step(ins)
                act("folded_v")
                for d in range(NL):
                    act(f"lag_w{d // 2}")
                    if d >= 3:
                        dve(f"lag_dots{d - 3}")
                    for half in range(2):
                        ins = nc.tensor.matmul(bank[2 + d % 3][0:C, half * QK:(half + 1) * QK],
                                               lagw[:, d, half * C:(half + 1) * C], w_fold[:, :],
                                               start=True, stop=True)
                    step(ins)
                dve("ring_taps")
                pe.wait_ge(edges_taken[0], (b + 1) * NIT)
                pe.wait_ge(edges_taken[1], (b + 1) * NIT)
                pe.wait_ge(edge_rows_loaded, (b + 1) * 32)

                def ring_dots(j):
                    act(f"ring{j}")
                    side, _ = EDGE_N[j]
                    n = EP if side < 2 else 128
                    for half in range(2):
                        ins = nc.tensor.matmul(acc[0][0:C, half * QK:(half + 1) * QK],
                                               ring_sb[0:n, j % 2, half * C:(half + 1) * C], ring_sb[0:n, j % 2, :],
                                               start=(j == 0 and half == 0), stop=(j == len(EDGE_N) - 1),
                                               skip_group_check=True)
                    return ins

                act("lags2")
                dve("lags0")
                for j, (side, piece) in enumerate(EDGE_N):
                    n = EP if side < 2 else 128
                    if j >= 2:
                        act(f"ring{j - 2}")
                    for t in range(3):
                        if side < 2:
                            src = edge_rows[:, side, piece * EP + t:piece * EP + t + EP]
                            tap = (1 - side) * 6 + t
                        else:
                            src = edge_cols[:, side - 2, piece * 128 + t:piece * 128 + t + 128]
                            tap = 3 * t + (3 - side) * 2
                        ins = nc.tensor.matmul(bank[j % 2][0:n, 0:QK], src, ring_w[:, tap, :],
                                               start=(t == 0), stop=(t == 2))
                    step(ins)
                    if j >= 1:
                        ring_dots(j - 1)
                step(ring_dots(len(EDGE_N) - 1))
                dve("dots_ring")
                step(nc.tensor.transpose(small[0:C, 0:C], dots2[:, C:QK], ident_c))
                dve("dots_k")
                step(nc.tensor.transpose(small[0:C, 0:C], att[:, 1, :], ident_c))
                dve("attn")
                step(nc.tensor.matmul(small[0:C, 0:C], att[:, 4, :], w_projT[:, :], start=True, stop=True))
                dve("v_taps")
                step(nc.tensor.matmul(bank[2][0:K1, 0:5 * C], v_fold[:, :], v_taps[:, 0:5, :], start=True, stop=True))
                step(nc.tensor.matmul(bank[3][0:K1, 0:4 * C], v_fold[:, :], v_taps[:, 5:9, :], start=True, stop=True))
                dve("conv_5")

                def two_rows(i, q, first=False, last=False):
                    o = bank[q % 4]
                    taps = [4, 0, 1, 2, 3, 5, 6, 7, 8]
                    for t in taps:
                        dy, dx = t // 3, t % 3
                        a, n = 0, 2
                        if first and dy == 0:
                            a, n = 1, 1
                        if last and dy == 2:
                            n = 1
                        row = 2 * q + dy + a
                        ins = nc.tensor.matmul(o[0:C, a * W:(a + n) * W], conv_w[:, t, :],
                                               xc[i][:, row:row + n, 1 + dx:1 + dx + W],
                                               start=(t == 4), stop=(t == 8), skip_group_check=True)
                    ins.then_inc(x1_ready, 1)

                def conv_chunk(k, i, first=False, last=False):
                    pe.wait_ge(x_loaded[i], b * 16 * NZ + (NIT + 1) * 16 + k * 16)
                    for q in range(CH // 2):
                        if not (first and i == 0 and q < 4):
                            pe.wait_ge(x1_copied, b * PAIRS + k * CH + i * CH // 2 + q - 3)
                        two_rows(i, q, first and i == 0 and q == 0, last and i == 1 and q == CH // 2 - 1)

                for i in range(2):
                    conv_chunk(0, i, first=True)
                with pe.Fori(1, NIT - 1) as k:
                    for i in range(2):
                        conv_chunk(k, i)
                for i in range(2):
                    conv_chunk(NIT - 1, i, last=True)

                pe.wait_ge(x1_copied, (b + 1) * PAIRS)
                dve("second1")
                step(nc.tensor.matmul(small[0:C, 0:2], const_("avg_mean", C), st1[:, :], start=True, stop=True))
                dve("pooled")
                step(nc.tensor.matmul(small[0:RED, 0:1], w_1T[:, :], gm1[:, 6:7], start=True, stop=True))
                act("gate")
                for t in range(TAPS):
                    ins = nc.tensor.matmul(small[0:C, t:t + 1], w_2T[:, t, :], hid[:, :], start=True, stop=True)
                step(ins)
                dve("columns")
                step(nc.tensor.matmul(small[0:CG * SR, 0:NG * NV], const_("spread_in", C), cols1[:, :, :],
                                      start=True, stop=True))
                step(nc.tensor.matmul(bank[3][0:CG * SO, 0:NG], const_("spread_out", C), cols1[:, :, NV - 1],
                                      start=True, stop=True))

                with pe.Fori(0, NGI) as g:
                    dve("strip_means")
                    act("bias_spread")
                    for i in range(2):
                        pe.wait_ge(band_step, (b * NG + g * 2 + i + 1) * TAPS)
                        for u in range(YU):
                            j = (i * YU + u) % 5
                            n = min(2, NS - 2 * u)
                            pe.wait_ge(y_copied[j], b * NG + g * 2 + i)
                            for dx in range(3):
                                ins = nc.tensor.matmul(bank[j][0:CG * SO, 0:n * W], bands[i][:, dx, :],
                                                       xs[i][:, 2 * u:2 * u + n, dx:dx + W],
                                                       start=(dx == 0), stop=(dx == 2))
                            ins.then_inc(y_ready, 1)

        @block.vector
        def _(dve):
            dve.wait_ge(setup_loaded, 16 * SETUP_DMAS)
            for d in range(NL):
                dve.wait_ge(setup_pe, d + 1)
                nc.vector.tensor_scalar(lag_coef[:, d, :], bank[d % 5][0:C, 0:2 * QK], 0.5 if d == 0 else 1.0, None,
                                        ALU.mult).then_inc(setup_dve, 1)
            nc.vector.tensor_scalar(bn_sb[:, 2:3], bn_in[:, 3:4], BN_EPS, None, ALU.add).then_inc(setup_dve, 1)
            dve.wait_ge(setup_act, 1)
            nc.vector.reciprocal(bn_sb[:, 2:3], bn_sb[:, 3:4]).then_inc(setup_dve, 1)
            dve.wait_ge(setup_dve, NL + 2)
            nc.vector.tensor_tensor(bn_sb[:, 0:1], bn_sb[:, 2:3], bn_in[:, 0:1], ALU.mult).then_inc(setup_dve, 1)
            dve.wait_ge(setup_dve, NL + 3)
            nc.vector.tensor_tensor(bn_sb[:, 3:4], bn_sb[:, 0:1], bn_in[:, 2:3], ALU.mult).then_inc(setup_dve, 1)
            dve.wait_ge(setup_dve, NL + 4)
            nc.vector.tensor_tensor(bn_sb[:, 1:2], bn_in[:, 1:2], bn_sb[:, 3:4], ALU.subtract).then_inc(setup_dve, 1)
            dve.wait_ge(setup_dve, NL + 5)
            ident_c = const_("ident", C)[:, 0:C]
            small = bank[4]
            with dve.Fori(0, B) as b:
                def after(name):
                    dve.wait_ge(dve_step, b * NDVE + at(DVE_STEPS, name))

                def pe(name):
                    dve.wait_ge(pe_step, b * NPE + at(PE_STEPS, name))

                def act(name):
                    dve.wait_ge(act_step, b * NACT + at(ACT_STEPS, name))

                def step(ins):
                    ins.then_inc(dve_step, 1)

                def group_scale(gm, mom, tag, pe_name, act_name):
                    pe(pe_name)
                    step(nc.vector.tensor_copy(gm[:, 0:1], mom[:, 0:1]))
                    after("mean" + tag)
                    step(nc.vector.tensor_tensor(gm[:, 1:2], gm[:, 0:1], gm[:, 0:1], ALU.mult))
                    after("meansq" + tag)
                    step(nc.vector.tensor_tensor(gm[:, 2:3], mom[:, 1:2], gm[:, 1:2], ALU.subtract))
                    after("var" + tag)
                    step(nc.vector.tensor_scalar(gm[:, 3:4], gm[:, 2:3], 0.0, GN_EPS, ALU.max, ALU.add))
                    act(act_name)
                    step(nc.vector.reciprocal(gm[:, 5:6], gm[:, 4:5]))

                dve.wait_ge(lags_summed, b + 1)
                step(nc.vector.tensor_copy(lags[:, 0, 0:3 * K1], acc[0][0:K1, 0:3 * K1]))
                after("lags0")
                step(nc.vector.tensor_tensor(sq0[:, :], lags[0:C, 0, 0:C], ident_c, ALU.mult))
                step(nc.vector.tensor_copy(st0[:, 0:1], lags[0:C, 0, C:K1]))
                after("squares0")
                step(nc.vector.reduce_sum(st0[:, 1:2], sq0[:, :], AX))
                group_scale(gm0, small[0:C, 0:2], "0", "means0", "std0")
                after("rstd0")
                step(nc.vector.tensor_scalar(fold[:, 0:C], ident_c, gm0[:, 5:6], None, ALU.mult))
                step(nc.vector.tensor_scalar(fold[:, C:K1], gm0[:, 0:1], gm0[:, 5:6], -1.0, ALU.mult, ALU.mult))
                pe("folded")
                step(nc.vector.tensor_copy(w_fold[:, :], bank[2][0:K1, 0:QK]))
                after("folded_qk")
                step(nc.vector.tensor_tensor(ring_w, w_fold[:, :].unsqueeze(1).to_broadcast([K1, TAPS, QK]),
                                             dw_all[:, :, :], ALU.mult))
                for d in range(NL):
                    pe(f"lag_qk{d}")
                    step(nc.vector.tensor_tensor(dots_all[:, d, :], bank[2 + d % 3][0:C, 0:2 * QK], lag_coef[:, d, :],
                                                 ALU.mult))
                after(f"lag_dots{NL - 1}")
                step(nc.vector.reduce_sum(dots[:, :], dots_all.rearrange("p d a -> p a d"), AX))
                pe("ring_qk")
                after("dots")
                step(nc.vector.scalar_tensor_tensor(dots2[:, :], acc[0][0:C, 0:2 * QK], -0.5, dots[:, :],
                                                    ALU.mult, ALU.add))
                after("dots_ring")
                own_in = dots2[:, :].rearrange("p (a c) -> p a c", c=C)[:, 0:4:3, :]
                step(nc.vector.tensor_tensor(own[:, :, :], own_in, ident_c.unsqueeze(1).to_broadcast([C, 2, C]),
                                             ALU.mult))
                after("own")
                step(nc.vector.reduce_sum(nrm[:, 0:2], own[:, :, :], AX))
                after("own_sum")
                step(nc.vector.tensor_scalar(nrm[:, 2:4], nrm[:, 0:2], 2.0, NORM_EPS ** 2, ALU.mult, ALU.max))
                act("norm")
                step(nc.vector.reciprocal(nrm[:, 6:8], nrm[:, 4:6]))
                after("norm_inv")
                step(nc.vector.tensor_scalar(nrm[:, 8:9], nrm[:, 6:7], HD ** -0.5, None, ALU.mult))
                pe("dots_t")
                step(nc.vector.tensor_tensor(att[:, 0, :], small[0:C, 0:C], dots2[:, QK:QK + C], ALU.add))
                after("dots_kq")
                step(nc.vector.tensor_scalar(att[:, 1, :], att[:, 0, :], nrm[:, 7:8], None, ALU.mult))
                pe("logits")
                step(nc.vector.scalar_tensor_tensor(att[:, 2, :], small[0:C, 0:C], nrm[:, 8:9],
                                                    const_("off_head", C), ALU.mult, ALU.add))
                after("masked")
                step(nc.vector.reduce_max(nrm[:, 9:10], att[:, 2, :], AX))
                after("max")
                step(nc.vector.tensor_scalar(nrm[:, 0:1], nrm[:, 9:10], -1.0, None, ALU.mult))
                act("exp")
                step(nc.vector.reciprocal(nrm[:, 2:3], nrm[:, 1:2]))
                after("sum_inv")
                step(nc.vector.tensor_scalar(att[:, 4, :], att[:, 3, :], nrm[:, 2:3], None, ALU.mult))
                pe("attn_proj")
                step(nc.vector.tensor_tensor(v_taps, small[0:C, 0:C].unsqueeze(1).to_broadcast([C, TAPS, C]),
                                             v_dw[:, :].unsqueeze(2).to_broadcast([C, TAPS, C]), ALU.mult))
                pe("conv_a")
                step(nc.vector.tensor_copy(conv_w[:, 0:4, :], bank[2][0:K1, 0:4 * C]))
                step(nc.vector.tensor_tensor(conv_w[:, 4, :], bank[2][0:K1, 4 * C:5 * C],
                                             const_("ident", K1)[:, 0:C], ALU.add))
                pe("conv_b")
                step(nc.vector.tensor_copy(conv_w[:, 5:9, :], bank[3][0:K1, 0:4 * C]))

                with dve.Fori(0, NIT) as k:
                    for i in range(2):
                        for q in range(CH // 2):
                            dve.wait_ge(x1_copied, b * PAIRS + k * CH + i * CH // 2 + q + 1)
                            ins = nc.vector.bn_stats(x1_stats[:, bass.ds(k * CH + i * CH // 2 + q, 1), :],
                                                     stage[i][0:C, 2 * q * W:(2 * q + 2) * W])
                        ins.then_inc(x1_counted[i], 1)
                dve.wait_ge(x1_counted[1], (b + 1) * NIT)
                step(nc.vector.memset(vec1[:, :], 0.0))
                step(nc.vector.bn_aggr(mv1[:, :], x1_stats[:, :, :]))
                after("channel1")
                step(nc.vector.tensor_copy(st1[:, 0:1], mv1[:, 0:1]))
                step(nc.vector.tensor_tensor(gm1[:, 7:8], mv1[:, 0:1], mv1[:, 0:1], ALU.mult))
                after("mean_sq1")
                step(nc.vector.tensor_tensor(st1[:, 1:2], mv1[:, 1:2], gm1[:, 7:8], ALU.add))
                group_scale(gm1, small[0:C, 0:2], "1", "means1", "std1")
                after("rstd1")
                step(nc.vector.tensor_scalar(gm1[:, 6:7], mv1[:, 0:1], gm1[:, 0:1], gm1[:, 5:6],
                                             ALU.subtract, ALU.mult))
                pe("dynamic")
                step(nc.vector.tensor_tensor(dyn[:, :], small[0:C, 0:TAPS], b_2[:, :], ALU.add))
                after("dyn_b2")
                step(nc.vector.tensor_scalar(vec1[:, 0:TAPS], dyn[:, :], gm1[:, 5:6], None, ALU.mult))
                after("taps1")
                step(nc.vector.tensor_scalar(vec1[:, 4:5], vec1[:, 4:5], 1.0, None, ALU.add))
                step(nc.vector.tensor_copy(vec1[:, TAPS:TAPS + 1], gm1[:, 0:1]))
                step(nc.vector.tensor_tensor(vec1[:, TAPS + 1:NV], gm1[:, 0:1], b_out[:, :], ALU.add))
                after("col_bias")
                step(nc.vector.tensor_tensor(cols1[:, :, :], const_("group_of", C).unsqueeze(2).to_broadcast([C, NG, NV]),
                                             vec1[:, :].unsqueeze(1).to_broadcast([C, NG, NV]), ALU.mult))
                pe("spread")
                step(nc.vector.tensor_copy(taps1[:, :, :].rearrange("p g n -> p (g n)"), small[0:CG * SR, 0:NG * NV]))
                after("taps_spread")
                step(nc.vector.tensor_tensor(means1[:, :, :], taps1[:, :, TAPS:TAPS + 1].to_broadcast([CG * SR, NG, 3]),
                                             const_("strip_rows", 128).unsqueeze(1).to_broadcast([CG * SR, NG, 3]),
                                             ALU.mult))
                with dve.Fori(0, NGI) as g:
                    after("strip_means")
                    for i in range(2):
                        done = b * NG + g * 2 + i
                        dve.wait_ge(xs_loaded[i], (b * NGI + g + 1) * 16 * CG)
                        for n, (s0, s1) in enumerate(((0, 1), (1, NS - 1), (NS - 1, NS))):
                            part = xs[i][:, s0:s1, 1:1 + W]
                            nc.vector.tensor_scalar(part, part, means1[:, bass.ds(g * 2 + i, 1), n], None,
                                                    ALU.subtract).then_inc(xs_centred, 1)
                        for dy in range(3):
                            if dy:
                                dve.wait_ge(band_step, done * TAPS + 3 * dy)
                            mask = const_("band", 128)[:, dy * CG * SO:(dy + 1) * CG * SO]
                            for dx in range(3):
                                tap = taps1[:, bass.ds(g * 2 + i, 1), 3 * dy + dx]
                                if dy == 0:
                                    ins = nc.vector.tensor_scalar(bands[i][:, dx, :], mask, tap, None, ALU.mult)
                                else:
                                    ins = nc.vector.scalar_tensor_tensor(bands[i][:, dx, :], mask, tap,
                                                                         bands[i][:, dx, :], ALU.mult, ALU.add)
                                ins.then_inc(band_step, 1)

        @block.scalar
        def _(eng):
            eng.wait_ge(setup_dve, NL + 1)
            nc.scalar.activation(bn_sb[:, 3:4], bn_sb[:, 2:3], ACT.Sqrt).then_inc(setup_act, 1)
            with eng.Fori(0, B) as b:
                def pe(name):
                    eng.wait_ge(pe_step, b * NPE + at(PE_STEPS, name))

                def dve(name):
                    eng.wait_ge(dve_step, b * NDVE + at(DVE_STEPS, name))

                def step(ins):
                    ins.then_inc(act_step, 1)

                def copy(dst, src):
                    return nc.scalar.activation(dst, src, ACT.Copy)

                with eng.Fori(0, NIT) as k:
                    for r in range(RING):
                        eng.wait_ge(row_turned, b * H + k * RING + r + 1)
                        copy(xt[:, r, :, :].rearrange("p s c -> p (s c)"), bank[r % 2][:, 0:4 * K1]).then_inc(row_kept, 1)
                eng.wait_ge(lags_summed, b + 1)
                for dx in (1, 2):
                    step(copy(lags[:, dx, :], acc[dx][0:K1, 0:LAG_W]))
                dve("vareps0")
                step(nc.scalar.activation(gm0[:, 4:5], gm0[:, 3:4], ACT.Sqrt))
                pe("folded_v")
                step(copy(v_fold[:, :], bank[3][0:C, 0:K1]))
                for j in range(7):
                    pe(f"lag_w{j}")
                    n = min(2, NL - 2 * j)
                    step(copy(lagw[:, 2 * j:2 * j + n, :].rearrange("p d a -> p (d a)"), bank[j % 2][0:K1, 0:n * QK]))
                for j, (side, _) in enumerate(EDGE_N):
                    n = EP if side < 2 else 128
                    pe(f"ring{j}")
                    step(copy(ring_sb[0:n, j % 2, :], bank[j % 2][0:n, 0:QK]))
                dve("norm_sq")
                step(nc.scalar.activation(nrm[:, 4:6], nrm[:, 2:4], ACT.Sqrt))
                dve("max_neg")
                step(nc.scalar.activation(att[:, 3, :], att[:, 2, :], ACT.Exp, bias=nrm[:, 0:1],
                                          accum_out=nrm[:, 1:2]))
                for i in range(2):
                    eng.wait_ge(y_stored[i], b * NGI * 16 * 2 * CG)
                with eng.Fori(0, NIT) as k:
                    for i in range(2):
                        eng.wait_ge(x1_stored[i], (b * NIT + k) * 16)
                        eng.wait_ge(x1_counted[i], b * NIT + k)
                        for q in range(CH // 2):
                            eng.wait_ge(x1_ready, b * PAIRS + k * CH + i * CH // 2 + q + 1)
                            copy(x1_out[i][:, 2 * q:2 * q + 2, :].rearrange("p r w -> p (r w)"),
                                 bank[q % 4][0:C, :]).then_inc(x1_copied, 1)
                        eng.wait_ge(x1_copied, b * PAIRS + k * CH + (i + 1) * CH // 2)
                        eng.dma_start(x1_dram[:, bass.ds(k * 2 * CH + i * CH + 1, CH), :], x1_out[i][:, :, :]).then_inc(
                            x1_stored[i], 16)
                dve("vareps1")
                step(nc.scalar.activation(gm1[:, 4:5], gm1[:, 3:4], ACT.Sqrt))
                pe("hidden")
                step(nc.scalar.activation(hid[:, :], bank[4][0:RED, 0:1], ACT.Sigmoid, bias=bn_sb[:, 1:2],
                                          scale=bn_sb[:, 0:1]))
                pe("spread_bias")
                step(copy(bias1[:, :], bank[3][0:CG * SO, 0:NG]))
                eng.wait_ge(act_step, (b + 1) * NACT)
                copy(spare[:, :], bias1[:, 0:2])
                with eng.Fori(0, NGI) as g:
                    for i in range(2):
                        nc.scalar.activation(bias_g[:, i:i + 1], bias1[:, bass.ds(g * 2 + i, 1)], ACT.Copy).then_inc(
                            bias_taken, 1)
                        eng.wait_ge(bias_taken, b * NG + g * 2 + i + 1)
                        eng.wait_ge(y_stored[i], (b * NGI + g) * 16 * 2 * CG)
                        for u in range(YU):
                            n = min(2, NS - 2 * u)
                            eng.wait_ge(y_ready, (b * NG + g * 2 + i) * YU + u + 1)
                            nc.scalar.activation(ys[i][:, 2 * u:2 * u + n, :].rearrange("p r w -> p (r w)"),
                                                 bank[u][0:CG * SO, 0:n * W], ACT.Identity,
                                                 bias=bias_g[:, i:i + 1]).then_inc(y_copied[u], 1)
                        for u in range(YU):
                            eng.wait_ge(y_copied[u], b * NG + g * 2 + i + 1)
                        for c in range(CG):
                            at_c = b * (C * H * W) + g * (2 * CG * H * W) + (i * CG + c) * H * W
                            eng.dma_start(bass.AP(out.tensor, at_c, [[W, SO], [SO * W, NS - 1], [1, W]]),
                                          ys[i][c * SO:(c + 1) * SO, 0:NS - 1, :]).then_inc(y_stored[i], 16)
                            eng.dma_start(bass.AP(out.tensor, at_c + (NS - 1) * SO * W, [[W, LAST], [1, W]]),
                                          ys[i][c * SO:c * SO + LAST, NS - 1, :]).then_inc(y_stored[i], 16)


def kernel(x, L0_conv_qkv_w, L0_conv_qkv_dw_w, L0_conv_proj_w, L1_conv_w1, L1_conv_gamma, L1_conv_beta,
           L1_conv_running_mean, L1_conv_running_var, L1_conv_w2, L1_conv_b2, L1_conv_bias):
    import concourse.bacc as bacc
    from concourse.bass_utils import run_bass_kernel_spmd

    dw = np.asarray(L0_conv_qkv_dw_w).reshape(3 * C, TAPS)
    dw_t = dw[0:QK].T
    lag_t = np.zeros((TAPS, NL, QK), np.float32)
    for d, (dx, dy) in enumerate(LAGS):
        for t in range(TAPS):
            ty, tx = t // 3 + dy, t % 3 + dx
            if 0 <= ty < 3 and 0 <= tx < 3:
                lag_t[t, d] = dw_t[ty * 3 + tx]
    arrays = {
        "x": np.asarray(x),
        "qkv_wT": np.asarray(L0_conv_qkv_w)[:, :, 0, 0].T,
        "dw_t": dw_t,
        "lag_t": lag_t,
        "dw_rep": np.broadcast_to(dw_t, (K1, TAPS, QK)),
        "dw_v": dw[QK:],
        "proj_wT": np.asarray(L0_conv_proj_w)[:, :, 0, 0].T,
        "w1T": np.asarray(L1_conv_w1).T,
        "bn": np.stack([np.asarray(a) for a in (L1_conv_gamma, L1_conv_beta, L1_conv_running_mean,
                                                L1_conv_running_var)], 1),
        "w2T": np.asarray(L1_conv_w2).reshape(C, TAPS, RED).transpose(2, 1, 0),
        "b2": np.asarray(L1_conv_b2).reshape(C, TAPS),
        "bias": np.asarray(L1_conv_bias).reshape(C, 1),
        "const": constants(),
    }
    arrays = {f"in_{name}": np.ascontiguousarray(a) for name, a in arrays.items()}
    nc = bacc.Bacc("TRN2", target_bir_lowering=False, num_devices=1)
    args = [nc.dram_tensor(name, a.shape, mybir.dt.from_np(a.dtype), kind="ExternalInput").ap()
            for name, a in arrays.items()]
    out = nc.dram_tensor("out", (B, C, H, W), mybir.dt.float32, kind="ExternalOutput").ap()
    build(nc, *args, out)
    result = run_bass_kernel_spmd(nc, [arrays], core_ids=[0])
    return result.results[0]["out"]
```

```python
from contextlib import ExitStack

import numpy as np

import concourse.bass as bass
from concourse import mybir

B, C, H, W = 8, 96, 256, 256
HEADS = 6
HD = C // HEADS
GN_GROUPS = 32
CPG = C // GN_GROUPS
RED = 24
K1 = C + 1
K2 = K1 + 1
QK = 2 * C
GN_EPS = 1e-5
BN_EPS = 1e-5
NORM_EPS = 1e-12
TAPS = 9

WP = W + 4
WB = W + 2
U = 8
UK = 4
NK = H // (U * UK)
RK = U * UK
NU = H // U
RING = 16
LAG = 6
LAGS = [(0, dy) for dy in range(3)] + [(dx, dy) for dx in (1, 2) for dy in range(-2, 3)]
NL = len(LAGS)
LAG_W = 5 * K2
V_TAPS = (1, 2, 3, 5, 6, 7, 8)
Y_TAPS = tuple(range(1, TAPS))

CG = 4
BL = 128 // CG
NG = C // CG
GK = NG // NK
NV = TAPS + 2
NP = NV + 2
PAIRS = H // 2
UP = U // 2
EDGES = [(i, n) for i in range(2) for n in range(3)] + [(i, n) for i in (2, 3) for n in range(2)]
EP = (W + 2) // 3

UNIT_OPS = "vvvyvvyvvyyyy"
assert UNIT_OPS.count("v") == len(V_TAPS) and UNIT_OPS.count("y") * UK == GK * len(Y_TAPS)

COLS = {}
_at = 0
for _name, _n in (("ident", 128), ("avg_sum", C), ("spread", 128), ("group_of", NG), ("off_head", C),
                  ("inside", 2), ("zero", 256)):
    COLS[_name] = (_at, _at + _n)
    _at += _n
NCONST = _at


def constants():
    t = np.zeros((128, NCONST), np.float32)

    def part(name):
        a, b = COLS[name]
        return t[:, a:b]

    part("ident")[:] = np.eye(128)
    c = np.arange(C)
    part("avg_sum")[:C] = (c[:, None] // CPG == c[None] // CPG) / (CPG * H * W)
    part("spread")[:C] = c[:, None] % CG == np.arange(128)[None] // BL
    part("group_of")[:C] = c[:, None] // CG == np.arange(NG)[None]
    part("off_head")[:C] = np.where(c[:, None] // HD == c[None] // HD, 0.0, -1e30)
    block = np.arange(128) % BL
    part("inside")[:, 0] = block > 0
    part("inside")[:, 1] = block < BL - 1
    return t


PE_ATT = (["means0", "folded", "folded_vT", "folded_v"] + [f"lag_w{j}" for j in range(7)]
          + [f"lag_qk{d}" for d in range(NL)] + [f"ring{j}" for j in range(10)]
          + ["ring_qk", "dots_t", "logits", "attn_proj", "middle"])
DVE_ATT = (["lags0", "squares0", "sums0", "sumsq0", "mean0", "meansq0", "var0", "vareps0", "rstd0", "fold_diag0",
            "fold0", "folded_qk", "ring_taps"]
           + [f"lag_dots{d}" for d in range(NL)]
           + ["dots", "dots_ring", "own", "own_sum", "norm_sq", "norm_inv", "norm_q", "dots_kq", "dots_k",
              "masked", "max", "max_neg", "sum_inv", "attn", "out_w", "middle_tap", "middle_w"])
ACT_ATT = (["lags1", "lags2", "std0", "folded_vT", "folded_v"] + [f"lag_w{j}" for j in range(7)]
           + [f"ring{j}" for j in range(10)] + ["norm", "exp"])
PE_DYN = ["means1", "hidden", "dynamic", "spread"]
DVE_DYN = ["sums1", "mean1", "meansq1", "var1", "vareps1", "rstd1", "channel1", "pooled", "dyn_b2", "taps1",
           "taps1_res", "col_mean", "col_bias", "columns", "taps_spread", "edge_means"]
ACT_DYN = ["std1", "gate"]


def at(steps, name):
    return steps.index(name) + 1


def build(nc, x, qkv_wT, dw_t, lag_t, dw_rep, dw_v, proj_wT, w1T, bn, w2T, b2, bias, const, ends, out):
    f32 = mybir.dt.float32
    f32r = mybir.dt.float32r
    ALU = mybir.AluOpType
    ACT = mybir.ActivationFunctionType
    AX = mybir.AxisListType.X
    x1_dram = nc.dram_tensor("x1", [B, C * H + 2, W], f32, kind="Internal").ap()
    coef_dram = nc.dram_tensor("coef", [C, NL, 2 * QK], f32, kind="Internal").ap()
    N_PA, N_DA, N_AA = len(PE_ATT), len(DVE_ATT), len(ACT_ATT)
    N_PD, N_DD, N_AD = len(PE_DYN), len(DVE_DYN), len(ACT_DYN)

    with ExitStack() as ctx:
        def sb(name, shape, dt=f32):
            return ctx.enter_context(nc.sbuf_tensor(name, shape, dt))

        def sem(name):
            return ctx.enter_context(nc.semaphore(name))

        xc = [sb(f"lag_x_{n}", [K1, U, WP]) for n in "ab"]
        xt_hi = sb("xt_hi", [128, RING, 4, K2], f32r)
        xt_lo = sb("xt_lo", [128, RING, 4, K2], f32r)
        xp = [sb(f"conv_x_{n}", [K1, U + 1, W]) for n in "ab"]
        vb = [sb(f"v_rows_{n}", [C, U + 2, WB]) for n in "ab"]
        va = sb("v_sum", [128, U * W])
        v_sum = va[0:C, :].rearrange("p (r w) -> p r w", w=W)
        rows_out = sb("rows_out", [128, U * W])
        stage = rows_out[0:C, :].rearrange("p (r w) -> p r w", w=W)
        lags = rows_out[0:K1, 0:3 * LAG_W].rearrange("p (d a) -> p d a", d=3)
        strips = sb("x1_strips", [128, GK, U + 2, WB])
        xs = [strips[:, j, :, :] for j in range(GK)]
        results = sb("results", [128, GK, U, W])
        ys = [results[:, j, :, :] for j in range(GK)]
        strips_flat = strips[:, :, :, :].rearrange("p g r w -> p (g r w)")
        lag_coef = strips_flat[0:C, 0:NL * 2 * QK].rearrange("p (d a) -> p d a", d=NL)
        lagw = strips_flat[0:K1, 2 * (U + 2) * WB:2 * (U + 2) * WB + NL * QK].rearrange("p (d a) -> p d a", d=NL)
        assert NL * 2 * QK <= 2 * (U + 2) * WB and NL * QK <= (U + 2) * WB
        dots_all = results[:, :, :, :].rearrange("p g r w -> p (g r w)")[0:C, 0:NL * 2 * QK].rearrange(
            "p (d a) -> p d a", d=NL)
        ring_w = va[0:K1, 0:TAPS * QK].rearrange("p (t a) -> p t a", t=TAPS)
        ct = sb("constants", [128, NCONST])
        w_qkvT = sb("w_qkvT", [C, 3 * C])
        w_projT = sb("w_projT", [C, C])
        w_1T = sb("w_1T", [C, RED])
        w_2T = sb("w_2T", [RED, TAPS, C])
        b_2 = sb("b_2", [C, TAPS])
        b_out = sb("b_out", [C, 1])
        v_dw = sb("v_dw", [C, TAPS])
        bn_in = sb("bn_in", [RED, 4])
        bn_sb = sb("bn_scale_shift", [RED, 4])
        taps_qk = sb("taps_qk", [TAPS, QK])
        taps_lag = results[:, :, :, :].rearrange("p g r w -> p (g r w)")[0:TAPS, 0:NL * QK].rearrange(
            "p (d a) -> p d a", d=NL)
        edge_rows = sb("edge_rows", [K1, 2, WP])
        edge_cols = sb("edge_cols", [K1, 2, H + 2])
        mom_turn = sb("moments_turn", [C, 2, UK * UP])
        x1_mom = sb("x1_moments", [C, 2, PAIRS])
        dw_all = sb("dw_all", [K1, TAPS, QK])
        sq0 = sb("sq0", [C, C])
        st0 = sb("st0", [C, 2])
        gm0 = sb("gm0", [C, 6])
        fold = sb("fold", [C, K1])
        w_fold = sb("w_fold", [K1, QK])
        v_foldT = sb("v_foldT", [K1, C])
        v_fold = sb("v_fold", [C, K1])
        out_w = sb("out_w", [C, C])
        mid_tap = sb("mid_tap", [C, C])
        mid_w = sb("mid_w", [K1, C])
        ring_sb = sb("ring_sb", [128, 2, QK])
        dots = sb("dots", [C, 2 * QK])
        dots2 = sb("dots2", [C, 2 * QK])
        own = sb("own", [C, 2, C])
        nrm = sb("nrm", [C, 10])
        att = sb("att", [C, 5, C])
        st1 = sb("st1", [C, 2])
        gm1 = sb("gm1", [C, 8])
        hid = sb("hid", [RED, 1])
        dyn = sb("dyn", [C, TAPS])
        vec1 = sb("vec1", [C, NV])
        cols1 = sb("cols1", [C, NG, NV])
        par_all = sb("par_all", [128, NG, NP])
        par = sb("par", [128, GK, NP])

        def const_(name, parts):
            a, b = COLS[name]
            return ct[0:parts, a:b]

        def ps(name):
            return ctx.enter_context(nc.psum_tensor(name, [128, 512], f32))

        acc = [ps(f"lag_acc{i}") for i in range(3)]
        bank = [ps(f"bank{i}") for i in range(5)]
        v_bank, x1_bank = (bank[2], bank[3]), (bank[4], bank[2])

        setup_loaded = sem("setup_loaded")
        setup_zeros = sem("setup_zeros")
        setup_edges = sem("setup_edges")
        setup_pe, setup_dve, setup_act = sem("setup_pe"), sem("setup_dve"), sem("setup_act")
        coef_stored, coef_loaded = sem("coef_stored"), sem("coef_loaded")
        x_loaded = [sem(f"x_loaded_{n}") for n in "ab"]
        edge_rows_loaded = sem("edge_rows_loaded")
        edges_taken = sem("edges_taken")
        row_turned = sem("row_turned")
        row_hi, row_lo = sem("row_hi"), sem("row_lo")
        lags_summed = sem("lags_summed")
        xp_loaded = [sem(f"xp_loaded_{n}") for n in "ab"]
        xp_end_loaded = sem("xp_end_loaded")
        v_ready, v_kept = sem("v_ready"), sem("v_kept")
        v_topped = sem("v_topped")
        v_begun = sem("v_begun")
        v_tap = sem("v_tap")
        x1_ready, x1_copied = sem("x1_ready"), sem("x1_copied")
        x1_summed = sem("x1_summed")
        x1_stored = sem("x1_stored")
        pe_att, dve_att, act_att = sem("pe_att"), sem("dve_att"), sem("act_att")
        pe_dyn, dve_dyn, act_dyn = sem("pe_dyn"), sem("dve_dyn"), sem("act_dyn")
        pads_zeroed = sem("pads_zeroed")
        xs_loaded = [sem(f"xs_loaded_{j}") for j in range(GK)]
        par_taken = sem("par_taken")
        xs_centred = sem("xs_centred")
        y_begun = sem("y_begun")
        y_tap = sem("y_tap")
        y_stored = [sem(f"y_stored_{j}") for j in range(GK)]

        SETUP_DMAS = 12
        NVT, NYT = len(V_TAPS), len(Y_TAPS)
        VP = PAIRS + 1
        block = ctx.enter_context(nc.Block())

        def pipeline(eng, step):
            step(0, True, False, False)
            step(1, True, True, False)
            with eng.Fori(2, B) as s:
                step(s, True, True, True)
            step(B, False, True, True)
            step(B + 1, False, False, True)

        @block.sync
        def _(sp):
            for dst, src in ((ct[:, :], const), (w_qkvT[:, :], qkv_wT), (w_projT[:, :], proj_wT), (w_1T[:, :], w1T),
                             (w_2T[:, :, :], w2T), (b_2[:, :], b2), (b_out[:, :], bias), (v_dw[:, :], dw_v),
                             (bn_in[:, :], bn), (taps_qk[:, :], dw_t), (taps_lag, lag_t),
                             (dw_all[:, :, :], dw_rep)):
                sp.dma_start(dst, src).then_inc(setup_loaded, 16)
            sp.wait_ge(setup_loaded, 16 * SETUP_DMAS)
            for r in (0, C * H + 1):
                sp.dma_start(x1_dram[:, r, :], const_("zero", B)).then_inc(setup_edges, 16)
            sp.wait_ge(setup_dve, NL)
            sp.dma_start(coef_dram, lag_coef).then_inc(coef_stored, 16)
            sp.wait_ge(coef_stored, 16)
            sp.wait_ge(setup_zeros, 15)

            def step(s, lags_, conv, result):
                a, b = s, s - 1

                def lag_load(c, k=0):
                    unit = k * UK + c
                    before = c - 1 if isinstance(k, int) and k == 0 and c < 1 else None
                    free = a * NU if before is not None else a * NU + unit - 1
                    sp.wait_ge(row_turned, free * U)
                    sp.wait_ge(edges_taken, free)
                    rows = x[bass.ds(a, 1), :, :, :].rearrange("b c h w -> (b c) h w")
                    sp.dma_start(xc[c % 2][0:C, :, 2:2 + W], rows[:, bass.ds(unit * U, U), :]).then_inc(
                        x_loaded[c % 2], 16)

                def conv_load(c, k=0, last=False):
                    unit = k * UK + c
                    first = isinstance(k, int) and k == 0 and c < 1
                    sp.wait_ge(x1_ready, b * PAIRS if first else b * PAIRS + (unit - 1) * UP)
                    rows = x[bass.ds(b, 1), :, :, :].rearrange("b c h w -> (b c) h w")
                    n = U if last else U + 1
                    if last:
                        sp.dma_start(xp[c % 2][0:C, U, :], ends[1:K1, :]).then_inc(xp_end_loaded, 16)
                        sp.wait_ge(xp_end_loaded, (b + 1) * 16)
                    row = K1 if last else 0
                    sp.dma_start(xp[c % 2][C:K1, U, :], ends[row:row + 1, :]).then_inc(xp_loaded[c % 2], 16)
                    sp.dma_start(xp[c % 2][0:C, 0:n, :], rows[:, bass.ds(unit * U, n), :]).then_inc(
                        xp_loaded[c % 2], 16)

                def turn(k, last=False):
                    for c in range(UK):
                        if lags_:
                            lag_load(c, k)
                        if conv:
                            conv_load(c, k, last and c == UK - 1)

                if not (lags_ or conv):
                    return
                turn(0)
                if lags_:
                    for i in range(2):
                        if conv:
                            sp.wait_ge(pe_att, a * N_PA)
                        sp.dma_start(edge_rows[0:C, i, 2:2 + W],
                                     x[bass.ds(a, 1), :, i * (H - 1), :].rearrange("b c w -> (b c) w")).then_inc(
                                         edge_rows_loaded, 16)
                with sp.Fori(1, NK - 1) as k:
                    turn(k)
                turn(NK - 1, last=True)
                if lags_:
                    if result:
                        sp.wait_ge(y_tap, (s - 1) * NG * NYT)
                    sp.dma_start(lag_coef, coef_dram).then_inc(coef_loaded, 16)

            pipeline(sp, step)

        @block.gpsimd
        def _(pool):
            n = 0
            for borders in (xc[0][:, :, :], xc[1][:, :, :], xp[0][:, :, :], xp[1][:, :, :], edge_cols[:, :, :],
                            edge_rows[:, :, :], vb[0][:, :, :], vb[1][:, :, :], xt_hi[:, :, :, K1:K2].bitcast(f32),
                            xt_lo[:, :, :, K1:K2].bitcast(f32)):
                nc.gpsimd.memset(borders, 0.0).then_inc(setup_zeros, 1)
                n += 1
                pool.wait_ge(setup_zeros, n)
            for ones in (xc[0][C:K1, :, 2:2 + W], xc[1][C:K1, :, 2:2 + W], edge_rows[C:K1, :, 2:2 + W],
                         xp[0][C:K1, :, :], xp[1][C:K1, :, :]):
                nc.gpsimd.memset(ones, 1.0).then_inc(setup_zeros, 1)
                n += 1
                pool.wait_ge(setup_zeros, n)
            pool.wait_ge(setup_edges, 32)

            def step(s, lags_, conv, result):
                if not result:
                    return
                b = s - 2
                if conv:
                    pool.wait_ge(dve_att, (s - 1) * N_DA + at(DVE_ATT, "dots_ring"))
                for column in (0, WB - 1):
                    zeros = const_("zero", 128)[:, 0:GK * (U + 2)].rearrange("p (g r) -> p g r", g=GK)
                    nc.gpsimd.tensor_tensor(strips[:, :, :, column], zeros, zeros, ALU.add).then_inc(pads_zeroed, 1)
                pool.wait_ge(pads_zeroed, (s - 1) * 2)
                pool.wait_ge(x1_stored, (b + 1) * NU * 16)

                def load(j, k=0):
                    at_row = b * ((C * H + 2) * W) + (k * GK + j) * (CG * H * W)
                    pool.dma_start(xs[j][:, :, 1:1 + W], bass.AP(x1_dram.tensor, at_row,
                                                                 [[U * W, 128], [W, U + 2], [1, W]])).then_inc(
                                                                     xs_loaded[j], 16)

                def store(j, k):
                    pool.wait_ge(y_tap, (b * NG + k * GK + j + 1) * NYT)
                    at_row = b * (C * H * W) + (k * GK + j) * (CG * H * W)
                    pool.dma_start(bass.AP(out.tensor, at_row, [[U * W, 128], [1, U * W]]),
                                   ys[j].rearrange("p r w -> p (r w)")).then_inc(y_stored[j], 16)

                for j in range(GK):
                    load(j)
                with pool.Fori(0, NK - 1) as k:
                    for j in range(GK):
                        store(j, k)
                        load(j, k + 1)
                for j in range(GK):
                    store(j, NK - 1)

            pipeline(pool, step)
            for j in range(GK):
                pool.wait_ge(y_stored[j], 16 * NK * B)

        @block.tensor
        def _(pe):
            ident = const_("ident", K1)[:, 0:K1]
            ident_c = const_("ident", C)[:, 0:C]
            pe.wait_ge(setup_loaded, 16 * SETUP_DMAS)
            for d in range(NL):
                if d >= 5:
                    pe.wait_ge(setup_dve, d - 4)
                for half in range(2):
                    ins = nc.tensor.matmul(bank[d % 5][0:C, half * QK:(half + 1) * QK],
                                           taps_qk[:, half * C:(half + 1) * C], taps_lag[:, d, :],
                                           start=True, stop=True)
                ins.then_inc(setup_pe, 1)
            pe.wait_ge(setup_zeros, 15)
            pe.wait_ge(setup_dve, NL)

            def step(s, lags_, conv):
                a, b = s, s - 1

                def turn_row(k, r, first=False):
                    i = r // U % 2
                    if r % U == 0:
                        pe.wait_ge(x_loaded[i], a * (NU // 2) * 16 + k * (UK // 2) * 16 + (r // (2 * U) + 1) * 16)
                    if not (first and r < 2):
                        pe.wait_ge(row_lo, a * H + k * RK + r - 1)
                    for p in range(4):
                        ins = nc.tensor.transpose(bank[r % 2][:, p * K2:p * K2 + K1],
                                                  xc[i][:, r % U, 2 + p:2 + p + W - 1:2], ident)
                    ins.then_inc(row_turned, 1)

                def lag_row(r, lo, hi):
                    for p in range(2):
                        for dx in range(3):
                            first, e = (max(lo, 0), hi) if dx == 0 else (lo, hi)
                            base = 0 if dx == 0 else -2
                            for left, right in ((xt_hi, xt_hi), (xt_hi, xt_lo), (xt_lo, xt_hi)):
                                q = first
                                while q <= e:
                                    slot = (r + q) % RING
                                    n = min(e - q + 1, RING - slot)
                                    ins = nc.tensor.matmul(
                                        acc[dx][0:K1, (q - base) * K2:(q - base + n) * K2],
                                        left[:, r % RING, p, 0:K1], right[:, slot:slot + n, p + dx, :],
                                        start=False, stop=False, skip_group_check=True)
                                    q += n
                    return ins

                def v_pairs(c, k):
                    unit = k * UK + c
                    pe.wait_ge(xp_loaded[c % 2], b * NU * 16 + k * (UK * 16) + (c // 2 + 1) * 32)
                    for p in range(UP):
                        if p == 0:
                            pe.wait_ge(x1_copied, b * PAIRS + unit * UP)
                        elif p == 1:
                            pe.wait_ge(v_kept, b * VP + 1 + unit * UP)
                        else:
                            pe.wait_ge(v_kept, b * VP + 1 + unit * UP + p - 1)
                        nc.tensor.matmul(v_bank[p % 2][0:C, :], v_foldT[:, :], xp[c % 2][:, 1 + 2 * p:3 + 2 * p, :],
                                         start=True, stop=True).then_inc(v_ready, 1)

                def x1_pairs(c, k):
                    unit = k * UK + c
                    for p in range(UP):
                        if p == 0:
                            pe.wait_ge(x1_copied, b * PAIRS + unit * UP)
                        elif p == 1:
                            pe.wait_ge(v_kept, b * VP + 1 + unit * UP + UP)
                        else:
                            pe.wait_ge(x1_copied, b * PAIRS + unit * UP + p - 1)
                        o = x1_bank[p % 2][0:C, :]
                        nc.tensor.matmul(o, mid_w[:, :], xp[c % 2][:, 2 * p:2 * p + 2, :], start=True, stop=False)
                        if p == 0:
                            pe.wait_ge(v_tap, (b * NU + unit + 1) * NVT)
                        nc.tensor.matmul(o, out_w[:, :], v_sum[:, 2 * p:2 * p + 2, :], start=False,
                                         stop=True).then_inc(x1_ready, 1)

                def turn(k, first=False):
                    for c in range(UK):
                        if conv:
                            v_pairs(c, k)
                        if lags_:
                            for r in range(c * U, (c + 1) * U):
                                turn_row(k, r, first)
                                if not first:
                                    pe.wait_ge(row_lo, a * H + k * RK + r - LAG + 3)
                                    lag_row(r + RING - LAG, -2, 2)
                                elif r >= LAG:
                                    pe.wait_ge(row_lo, a * H + r - LAG + 3)
                                    lag_row(r - LAG, -min(r - LAG, 2), 2)
                        if conv:
                            x1_pairs(c, k)

                if lags_:
                    if conv:
                        pe.wait_ge(dve_att, a * N_DA)
                    for dx in range(3):
                        n = (3 if dx == 0 else 5) * K2
                        nc.tensor.matmul(acc[dx][0:K1, 0:n], const_("zero", 128)[:, 0:K1], ct[:, 0:n],
                                         start=True, stop=False, skip_group_check=True)
                if conv:
                    if not lags_:
                        pe.wait_ge(dve_att, s * N_DA)
                    pe.wait_ge(xp_loaded[0], b * NU * 16 + 32)
                    nc.tensor.matmul(x1_bank[0][0:C, 0:W], v_foldT[:, :], xp[0][:, 0, :], start=True,
                                     stop=True).then_inc(v_ready, 1)
                    pe.wait_ge(v_kept, b * VP + 1)
                if lags_:
                    turn(0, first=True)
                    with pe.Fori(1, NK) as k:
                        turn(k)
                else:
                    with pe.Fori(0, NK) as k:
                        turn(k)

                def dyn_step(ins):
                    ins.then_inc(pe_dyn, 1)

                def dve_d(name):
                    pe.wait_ge(dve_dyn, b * N_DD + at(DVE_DYN, name))

                def tail_row(q):
                    if lags_:
                        pe.wait_ge(row_lo, a * H + min(q + 3, H))
                        return lag_row(q % RING, -2, min(2, H - 1 - q))

                small = bank[3]
                for n in range(LAG):
                    ins = tail_row(H - LAG + n)
                    if conv and n == 1:
                        dve_d("sums1")
                        dyn_step(nc.tensor.matmul(small[0:C, 0:2], const_("avg_sum", C), st1[:, :], start=True,
                                                  stop=True))
                    if conv and n == 3:
                        dve_d("pooled")
                        dyn_step(nc.tensor.matmul(small[0:RED, 0:1], w_1T[:, :], gm1[:, 6:7], start=True, stop=True))
                    if conv and n == 4:
                        pe.wait_ge(act_dyn, b * N_AD + at(ACT_DYN, "gate"))
                        for t in range(TAPS):
                            i2 = nc.tensor.matmul(small[0:C, t:t + 1], w_2T[:, t, :], hid[:, :], start=True,
                                                  stop=True)
                        dyn_step(i2)
                if lags_:
                    ins.then_inc(lags_summed, 1)
                if conv:
                    dve_d("columns")
                    dyn_step(nc.tensor.matmul(small[:, 0:NG * NV], const_("spread", C), cols1[:, :, :],
                                              start=True, stop=True))
                    dve_d("edge_means")
                if lags_:
                    attention(a)

            def attention(b):
                def step(ins):
                    ins.then_inc(pe_att, 1)

                def dve(name):
                    pe.wait_ge(dve_att, b * N_DA + at(DVE_ATT, name))

                def act(name):
                    pe.wait_ge(act_att, b * N_AA + at(ACT_ATT, name))

                small = bank[4]
                dve("sumsq0")
                step(nc.tensor.matmul(small[0:C, 0:2], const_("avg_sum", C), st0[:, :], start=True, stop=True))
                dve("fold0")
                step(nc.tensor.matmul(bank[2][0:K1, 0:QK], fold[:, :], w_qkvT[:, 0:QK], start=True, stop=True))
                step(nc.tensor.matmul(bank[3][0:K1, 0:C], fold[:, :], w_qkvT[:, QK:3 * C], start=True, stop=True))
                step(nc.tensor.matmul(bank[3][0:C, C:C + K1], w_qkvT[:, QK:3 * C], fold[:, :], start=True, stop=True))
                dve("folded_qk")
                act("lags2")
                for j in range(7):
                    if j >= 2:
                        act(f"lag_w{j - 2}")
                    for d in range(2 * j, min(2 * j + 2, NL)):
                        dx, i = (0, d) if d < 3 else (1 + (d - 3) // 5, (d - 3) % 5)
                        ins = nc.tensor.matmul(bank[j % 2][0:K1, (d % 2) * QK:(d % 2 + 1) * QK],
                                               lags[:, dx, i * K2:i * K2 + K1], w_fold[:, :], start=True, stop=True)
                    step(ins)
                act("folded_v")
                for d in range(NL):
                    act(f"lag_w{d // 2}")
                    if d >= 3:
                        dve(f"lag_dots{d - 3}")
                    for half in range(2):
                        ins = nc.tensor.matmul(bank[2 + d % 3][0:C, half * QK:(half + 1) * QK],
                                               lagw[:, d, half * C:(half + 1) * C], w_fold[:, :],
                                               start=True, stop=True)
                    step(ins)
                dve("ring_taps")
                pe.wait_ge(edges_taken, (b + 1) * NU)
                pe.wait_ge(edge_rows_loaded, (b + 1) * 32)

                def ring_dots(j):
                    act(f"ring{j}")
                    side, _ = EDGES[j]
                    n = EP if side < 2 else 128
                    for half in range(2):
                        ins = nc.tensor.matmul(acc[0][0:C, half * QK:(half + 1) * QK],
                                               ring_sb[0:n, j % 2, half * C:(half + 1) * C], ring_sb[0:n, j % 2, :],
                                               start=(j == 0 and half == 0), stop=(j == len(EDGES) - 1),
                                               skip_group_check=True)
                    return ins

                act("lags2")
                dve("lags0")
                for j, (side, piece) in enumerate(EDGES):
                    n = EP if side < 2 else 128
                    if j >= 2:
                        act(f"ring{j - 2}")
                    for t in range(3):
                        if side < 2:
                            src = edge_rows[:, side, piece * EP + t:piece * EP + t + EP]
                            tap = (1 - side) * 6 + t
                        else:
                            src = edge_cols[:, side - 2, piece * 128 + t:piece * 128 + t + 128]
                            tap = 3 * t + (3 - side) * 2
                        ins = nc.tensor.matmul(bank[j % 2][0:n, 0:QK], src, ring_w[:, tap, :],
                                               start=(t == 0), stop=(t == 2))
                    step(ins)
                    if j >= 1:
                        ring_dots(j - 1)
                step(ring_dots(len(EDGES) - 1))
                dve("dots_ring")
                step(nc.tensor.transpose(small[0:C, 0:C], dots2[:, C:QK], ident_c))
                dve("dots_k")
                step(nc.tensor.transpose(small[0:C, 0:C], att[:, 1, :], ident_c))
                dve("attn")
                step(nc.tensor.matmul(small[0:C, 0:C], att[:, 4, :], w_projT[:, :], start=True, stop=True))
                dve("middle_tap")
                step(nc.tensor.matmul(bank[2][0:K1, 0:C], v_fold[:, :], mid_tap[:, :], start=True, stop=True))

            step(0, True, False)
            with pe.Fori(1, B) as s:
                step(s, True, True)
            step(B, False, True)

        @block.vector
        def _(dve):
            dve.wait_ge(setup_loaded, 16 * SETUP_DMAS)
            for d in range(NL):
                dve.wait_ge(setup_pe, d + 1)
                nc.vector.tensor_scalar(lag_coef[:, d, :], bank[d % 5][0:C, 0:2 * QK], 0.5 if d == 0 else 1.0, None,
                                        ALU.mult).then_inc(setup_dve, 1)
            nc.vector.tensor_scalar(bn_sb[:, 2:3], bn_in[:, 3:4], BN_EPS, None, ALU.add).then_inc(setup_dve, 1)
            dve.wait_ge(setup_act, 1)
            nc.vector.reciprocal(bn_sb[:, 2:3], bn_sb[:, 3:4]).then_inc(setup_dve, 1)
            dve.wait_ge(setup_dve, NL + 2)
            nc.vector.tensor_tensor(bn_sb[:, 0:1], bn_sb[:, 2:3], bn_in[:, 0:1], ALU.mult).then_inc(setup_dve, 1)
            dve.wait_ge(setup_dve, NL + 3)
            nc.vector.tensor_tensor(bn_sb[:, 3:4], bn_sb[:, 0:1], bn_in[:, 2:3], ALU.mult).then_inc(setup_dve, 1)
            dve.wait_ge(setup_dve, NL + 4)
            nc.vector.tensor_tensor(bn_sb[:, 1:2], bn_in[:, 1:2], bn_sb[:, 3:4], ALU.subtract).then_inc(setup_dve, 1)
            dve.wait_ge(setup_dve, NL + 5)
            ident_c = const_("ident", C)[:, 0:C]

            def step(s, lags_, conv, result):
                a, b, d = s, s - 1, s - 2

                def low_half(k, r):
                    dve.wait_ge(row_hi, a * H + k * RK + r + 1)
                    turned = bank[r % 2][:, 0:4 * K2].rearrange("p (s c) -> p s c", c=K2)[:, :, 0:K1]
                    nc.vector.tensor_tensor(xt_lo[:, r % RING, :, 0:K1], turned,
                                            xt_hi[:, r % RING, :, 0:K1].bitcast(f32), ALU.subtract).then_inc(row_lo, 1)

                def v_op(k, c, n):
                    unit = k * UK + c
                    if n == 0:
                        dve.wait_ge(v_begun, b * NU + unit + 1)
                    else:
                        dve.wait_ge(v_tap, (b * NU + unit) * NVT + n)
                    t = V_TAPS[n]
                    dy, dx = t // 3, t % 3
                    nc.vector.scalar_tensor_tensor(v_sum, vb[c % 2][:, dy:dy + U, dx:dx + W], v_dw[:, t:t + 1],
                                                   v_sum, ALU.mult, ALU.add).then_inc(v_tap, 1)

                def y_op(k, j, n):
                    group = d * NG + k * GK + j
                    if n == 0:
                        dve.wait_ge(y_begun, group + 1)
                    else:
                        dve.wait_ge(y_tap, group * NYT + n)
                    t = Y_TAPS[n]
                    dy, dx = t // 3, t % 3
                    nc.vector.scalar_tensor_tensor(ys[j], xs[j][:, dy:dy + U, dx:dx + W], par[:, j, t:t + 1],
                                                   ys[j], ALU.mult, ALU.add).then_inc(y_tap, 1)

                def turn(k):
                    if result:
                        dve.wait_ge(dve_dyn, (d + 1) * N_DD)
                        dve.wait_ge(par_taken, d * NK + k)
                        dve.wait_ge(y_tap, (d * NG + k * GK) * NYT)
                        nc.vector.tensor_scalar(par[:, :, :], par_all[:, bass.ds(k * GK, GK), :], 1.0, None,
                                                ALU.mult).then_inc(par_taken, 1)
                    ny = 0
                    for c in range(UK):
                        nv, row = 0, 0
                        for n, op in enumerate(UNIT_OPS):
                            while lags_ and row * len(UNIT_OPS) <= n * U:
                                low_half(k, c * U + row)
                                row += 1
                            if op == "v":
                                if conv:
                                    v_op(k, c, nv)
                                nv += 1
                            else:
                                if result:
                                    y_op(k, ny // NYT, ny % NYT)
                                ny += 1
                        assert not lags_ or row == U

                with dve.Fori(0, NK) as k:
                    turn(k)
                if conv:
                    dynamic(b)
                if lags_:
                    attention(a, result)

            def group_scale(gm, mom, tag, step, after, pe, act):
                pe("means" + tag)
                step(nc.vector.tensor_copy(gm[:, 0:1], mom[:, 0:1]))
                after("mean" + tag)
                step(nc.vector.tensor_tensor(gm[:, 1:2], gm[:, 0:1], gm[:, 0:1], ALU.mult))
                after("meansq" + tag)
                step(nc.vector.tensor_tensor(gm[:, 2:3], mom[:, 1:2], gm[:, 1:2], ALU.subtract))
                after("var" + tag)
                step(nc.vector.tensor_scalar(gm[:, 3:4], gm[:, 2:3], 0.0, GN_EPS, ALU.max, ALU.add))
                act("std" + tag)
                step(nc.vector.reciprocal(gm[:, 5:6], gm[:, 4:5]))

            def dynamic(b):
                def after(name):
                    dve.wait_ge(dve_dyn, b * N_DD + at(DVE_DYN, name))

                def pe(name):
                    dve.wait_ge(pe_dyn, b * N_PD + at(PE_DYN, name))

                def act(name):
                    dve.wait_ge(act_dyn, b * N_AD + at(ACT_DYN, name))

                def step(ins):
                    ins.then_inc(dve_dyn, 1)

                small = bank[3]
                dve.wait_ge(x1_summed, (b + 1) * NK)
                step(nc.vector.reduce_sum(st1[:, :], x1_mom[:, :, :], AX))
                group_scale(gm1, small[0:C, 0:2], "1", step, after, pe, act)
                step(nc.vector.tensor_scalar(gm1[:, 7:8], st1[:, 0:1], 1.0 / (H * W), gm1[:, 0:1],
                                             ALU.mult, ALU.subtract))
                after("channel1")
                step(nc.vector.tensor_tensor(gm1[:, 6:7], gm1[:, 7:8], gm1[:, 5:6], ALU.mult))
                pe("dynamic")
                step(nc.vector.tensor_tensor(dyn[:, :], small[0:C, 0:TAPS], b_2[:, :], ALU.add))
                after("dyn_b2")
                step(nc.vector.tensor_scalar(vec1[:, 0:TAPS], dyn[:, :], gm1[:, 5:6], None, ALU.mult))
                after("taps1")
                step(nc.vector.tensor_scalar(vec1[:, 4:5], vec1[:, 4:5], 1.0, None, ALU.add))
                step(nc.vector.tensor_scalar(vec1[:, TAPS:TAPS + 1], gm1[:, 0:1], -1.0, None, ALU.mult))
                step(nc.vector.tensor_tensor(vec1[:, TAPS + 1:NV], gm1[:, 0:1], b_out[:, :], ALU.add))
                after("col_bias")
                step(nc.vector.tensor_tensor(cols1[:, :, :], const_("group_of", C).unsqueeze(2).to_broadcast([C, NG, NV]),
                                             vec1[:, :].unsqueeze(1).to_broadcast([C, NG, NV]), ALU.mult))
                pe("spread")
                step(nc.vector.tensor_copy(par_all[:, :, 0:NV],
                                           small[:, 0:NG * NV].rearrange("p (g n) -> p g n", n=NV)))
                after("taps_spread")
                step(nc.vector.tensor_tensor(par_all[:, :, NV:NP],
                                             par_all[:, :, TAPS:TAPS + 1].to_broadcast([128, NG, 2]),
                                             const_("inside", 128).unsqueeze(1).to_broadcast([128, NG, 2]), ALU.mult))

            def attention(b, result):
                small = bank[4]

                def after(name):
                    dve.wait_ge(dve_att, b * N_DA + at(DVE_ATT, name))

                def pe(name):
                    dve.wait_ge(pe_att, b * N_PA + at(PE_ATT, name))

                def act(name):
                    dve.wait_ge(act_att, b * N_AA + at(ACT_ATT, name))

                def step(ins):
                    ins.then_inc(dve_att, 1)

                dve.wait_ge(lags_summed, b + 1)
                dve.wait_ge(x1_stored, b * NU * 16)
                step(nc.vector.tensor_copy(lags[:, 0, 0:3 * K2], acc[0][0:K1, 0:3 * K2]))
                after("lags0")
                step(nc.vector.tensor_tensor(sq0[:, :], lags[0:C, 0, 0:C], ident_c, ALU.mult))
                step(nc.vector.tensor_copy(st0[:, 0:1], lags[0:C, 0, C:K1]))
                after("squares0")
                step(nc.vector.reduce_sum(st0[:, 1:2], sq0[:, :], AX))
                group_scale(gm0, small[0:C, 0:2], "0", step, after, pe, act)
                after("rstd0")
                step(nc.vector.tensor_scalar(fold[:, 0:C], ident_c, gm0[:, 5:6], None, ALU.mult))
                step(nc.vector.tensor_scalar(fold[:, C:K1], gm0[:, 0:1], gm0[:, 5:6], -1.0, ALU.mult, ALU.mult))
                pe("folded")
                step(nc.vector.tensor_copy(w_fold[:, :], bank[2][0:K1, 0:QK]))
                after("folded_qk")
                step(nc.vector.tensor_tensor(ring_w, w_fold[:, :].unsqueeze(1).to_broadcast([K1, TAPS, QK]),
                                             dw_all[:, :, :], ALU.mult))
                dve.wait_ge(coef_loaded, (b + 1) * 16)
                if result:
                    for j in range(GK):
                        dve.wait_ge(y_stored[j], (b - 1) * NK * 16)
                for d in range(NL):
                    pe(f"lag_qk{d}")
                    step(nc.vector.tensor_tensor(dots_all[:, d, :], bank[2 + d % 3][0:C, 0:2 * QK], lag_coef[:, d, :],
                                                 ALU.mult))
                after(f"lag_dots{NL - 1}")
                step(nc.vector.reduce_sum(dots[:, :], dots_all.rearrange("p d a -> p a d"), AX))
                pe("ring_qk")
                after("dots")
                step(nc.vector.scalar_tensor_tensor(dots2[:, :], acc[0][0:C, 0:2 * QK], -0.5, dots[:, :],
                                                    ALU.mult, ALU.add))
                after("dots_ring")
                own_in = dots2[:, :].rearrange("p (a c) -> p a c", c=C)[:, 0:4:3, :]
                step(nc.vector.tensor_tensor(own[:, :, :], own_in, ident_c.unsqueeze(1).to_broadcast([C, 2, C]),
                                             ALU.mult))
                after("own")
                step(nc.vector.reduce_sum(nrm[:, 0:2], own[:, :, :], AX))
                after("own_sum")
                step(nc.vector.tensor_scalar(nrm[:, 2:4], nrm[:, 0:2], 2.0, NORM_EPS ** 2, ALU.mult, ALU.max))
                act("norm")
                step(nc.vector.reciprocal(nrm[:, 6:8], nrm[:, 4:6]))
                after("norm_inv")
                step(nc.vector.tensor_scalar(nrm[:, 8:9], nrm[:, 6:7], HD ** -0.5, None, ALU.mult))
                pe("dots_t")
                step(nc.vector.tensor_tensor(att[:, 0, :], small[0:C, 0:C], dots2[:, QK:QK + C], ALU.add))
                after("dots_kq")
                step(nc.vector.tensor_scalar(att[:, 1, :], att[:, 0, :], nrm[:, 7:8], None, ALU.mult))
                pe("logits")
                step(nc.vector.scalar_tensor_tensor(att[:, 2, :], small[0:C, 0:C], nrm[:, 8:9],
                                                    const_("off_head", C), ALU.mult, ALU.add))
                after("masked")
                step(nc.vector.reduce_max(nrm[:, 9:10], att[:, 2, :], AX))
                after("max")
                step(nc.vector.tensor_scalar(nrm[:, 0:1], nrm[:, 9:10], -1.0, None, ALU.mult))
                act("exp")
                step(nc.vector.reciprocal(nrm[:, 2:3], nrm[:, 1:2]))
                after("sum_inv")
                step(nc.vector.tensor_scalar(att[:, 4, :], att[:, 3, :], nrm[:, 2:3], None, ALU.mult))
                pe("attn_proj")
                step(nc.vector.tensor_copy(out_w[:, :], small[0:C, 0:C]))
                after("out_w")
                step(nc.vector.tensor_scalar(mid_tap[:, :], out_w[:, :], v_dw[:, 4:5], None, ALU.mult))
                pe("middle")
                step(nc.vector.tensor_tensor(mid_w[:, :], bank[2][0:K1, 0:C], const_("ident", K1)[:, 0:C], ALU.add))

            pipeline(dve, step)

        @block.scalar
        def _(eng):
            eng.wait_ge(setup_dve, NL + 1)
            nc.scalar.activation(bn_sb[:, 3:4], bn_sb[:, 2:3], ACT.Sqrt).then_inc(setup_act, 1)

            def copy(dst, src, **more):
                return nc.scalar.activation(dst, src, ACT.Copy, **more)

            def step(s, lags_, conv, result):
                a, b, d = s, s - 1, s - 2

                def high_half(k, r):
                    eng.wait_ge(row_turned, a * H + k * RK + r + 1)
                    turned = bank[r % 2][:, 0:4 * K2].rearrange("p (s c) -> p s c", c=K2)[:, :, 0:K1]
                    copy(xt_hi[:, r % RING, :, 0:K1], turned).then_inc(row_hi, 1)

                def outer_columns(k, c):
                    copy(edge_cols[:, :, bass.ds(1 + (k * UK + c) * U, U)],
                         xc[c % 2][:, :, 2:2 + W:W - 1].rearrange("p r e -> p e r")).then_inc(edges_taken, 1)

                def v_rows(k, c):
                    unit = k * UK + c
                    for p in range(UP):
                        eng.wait_ge(v_ready, b * VP + 1 + unit * UP + p + 1)
                        src = v_bank[p % 2][0:C, :].rearrange("p (r w) -> p r w", w=W)
                        if p == UP - 1:
                            copy(vb[(c + 1) % 2][:, 0:2, 1:1 + W], src)
                        copy(vb[c % 2][:, 2 + 2 * p:4 + 2 * p, 1:1 + W], src).then_inc(v_kept, 1)
                    eng.wait_ge(v_kept, b * VP + 1 + (unit + 1) * UP)
                    eng.wait_ge(x1_ready, b * PAIRS + unit * UP)
                    nc.scalar.activation(v_sum, vb[c % 2][:, 0:U, 0:W], ACT.Identity,
                                         scale=v_dw[:, 0:1]).then_inc(v_begun, 1)

                def x1_rows(k, c):
                    unit = k * UK + c
                    eng.wait_ge(x1_stored, (b * NU + unit) * 16)
                    for p in range(UP):
                        eng.wait_ge(x1_ready, b * PAIRS + unit * UP + p + 1)
                        src = x1_bank[p % 2][0:C, :]
                        copy(rows_out[0:C, 2 * p * W:(2 * p + 2) * W], src,
                             accum_out=mom_turn[:, 0, c * UP + p:c * UP + p + 1])
                        nc.scalar.activation(src, src, ACT.Square, accum_out=mom_turn[:, 1, c * UP + p:c * UP + p + 1]).then_inc(
                            x1_copied, 1)
                    eng.wait_ge(x1_copied, b * PAIRS + (unit + 1) * UP)
                    eng.dma_start(bass.AP(x1_dram.tensor, b * ((C * H + 2) * W) + W + unit * (U * W),
                                          [[H * W, C], [1, U * W]]),
                                  rows_out[0:C, :]).then_inc(x1_stored, 16)
                    if c == UK - 1:
                        copy(x1_mom[:, :, bass.ds(k * (UK * UP), UK * UP)], mom_turn[:, :, :]).then_inc(x1_summed, 1)

                def begin_group(k, j):
                    group = d * NG + k * GK + j
                    eng.wait_ge(xs_loaded[j], (d * NK + k + 1) * 16)
                    eng.wait_ge(par_taken, d * NK + k + 1)
                    for rows, scale, column in ((slice(0, 1), const_("inside", 128)[:, 0:1], NV),
                                                (slice(U + 1, U + 2), const_("inside", 128)[:, 1:2], NV + 1),
                                                (slice(1, U + 1), 1.0, TAPS)):
                        part = xs[j][:, rows, 1:1 + W]
                        nc.scalar.activation(part, part, ACT.Identity, scale=scale,
                                             bias=par[:, j, column:column + 1]).then_inc(xs_centred, 1)
                    eng.wait_ge(xs_centred, (group + 1) * 3)
                    eng.wait_ge(y_stored[j], (d * NK + k) * 16)
                    nc.scalar.activation(ys[j], xs[j][:, 0:U, 0:W], ACT.Identity, scale=par[:, j, 0:1],
                                         bias=par[:, j, TAPS + 1:NV]).then_inc(y_begun, 1)

                def turn(k):
                    for c in range(UK):
                        if conv:
                            v_rows(k, c)
                        if lags_:
                            high_half(k, c * U)
                            outer_columns(k, c)
                        if result and c < GK:
                            begin_group(k, c)
                        if lags_:
                            for r in range(c * U + 1, (c + 1) * U):
                                high_half(k, r)
                        if conv:
                            x1_rows(k, c)

                if conv:
                    eng.wait_ge(v_ready, b * VP + 1)
                    copy(vb[0][:, 1, 1:1 + W], x1_bank[0][0:C, 0:W]).then_inc(v_kept, 1)
                    copy(vb[0][:, 0, 1:1 + W], const_("zero", C)).then_inc(v_topped, 1)
                with eng.Fori(0, NK) as k:
                    turn(k)
                if conv:
                    eng.wait_ge(dve_dyn, b * N_DD + at(DVE_DYN, "vareps1"))
                    nc.scalar.activation(gm1[:, 4:5], gm1[:, 3:4], ACT.Sqrt).then_inc(act_dyn, 1)
                    eng.wait_ge(pe_dyn, b * N_PD + at(PE_DYN, "hidden"))
                    nc.scalar.activation(hid[:, :], bank[3][0:RED, 0:1], ACT.Sigmoid, bias=bn_sb[:, 1:2],
                                         scale=bn_sb[:, 0:1]).then_inc(act_dyn, 1)
                if lags_:
                    attention(a, result)

            def attention(b, result):
                def pe(name):
                    eng.wait_ge(pe_att, b * N_PA + at(PE_ATT, name))

                def dve(name):
                    eng.wait_ge(dve_att, b * N_DA + at(DVE_ATT, name))

                def step(ins):
                    ins.then_inc(act_att, 1)

                eng.wait_ge(lags_summed, b + 1)
                eng.wait_ge(x1_stored, b * NU * 16)
                for dx in (1, 2):
                    step(copy(lags[:, dx, :], acc[dx][0:K1, 0:LAG_W]))
                dve("vareps0")
                step(nc.scalar.activation(gm0[:, 4:5], gm0[:, 3:4], ACT.Sqrt))
                pe("folded_v")
                step(copy(v_foldT[:, :], bank[3][0:K1, 0:C]))
                step(copy(v_fold[:, :], bank[3][0:C, C:C + K1]))
                if result:
                    eng.wait_ge(y_tap, (b - 1) * NG * NYT)
                for j in range(7):
                    pe(f"lag_w{j}")
                    n = min(2, NL - 2 * j)
                    step(copy(lagw[:, 2 * j:2 * j + n, :].rearrange("p d a -> p (d a)"), bank[j % 2][0:K1, 0:n * QK]))
                for j, (side, _) in enumerate(EDGES):
                    n = EP if side < 2 else 128
                    pe(f"ring{j}")
                    step(copy(ring_sb[0:n, j % 2, :], bank[j % 2][0:n, 0:QK]))
                dve("norm_sq")
                step(nc.scalar.activation(nrm[:, 4:6], nrm[:, 2:4], ACT.Sqrt))
                dve("max_neg")
                step(nc.scalar.activation(att[:, 3, :], att[:, 2, :], ACT.Exp, bias=nrm[:, 0:1],
                                          accum_out=nrm[:, 1:2]))

            pipeline(eng, step)


def kernel(x, L0_conv_qkv_w, L0_conv_qkv_dw_w, L0_conv_proj_w, L1_conv_w1, L1_conv_gamma, L1_conv_beta,
           L1_conv_running_mean, L1_conv_running_var, L1_conv_w2, L1_conv_b2, L1_conv_bias):
    import concourse.bacc as bacc
    from concourse.bass_utils import run_bass_kernel_spmd

    dw = np.asarray(L0_conv_qkv_dw_w).reshape(3 * C, TAPS)
    dw_t = dw[0:QK].T
    lag_t = np.zeros((TAPS, NL, QK), np.float32)
    for d, (dx, dy) in enumerate(LAGS):
        for t in range(TAPS):
            ty, tx = t // 3 + dy, t % 3 + dx
            if 0 <= ty < 3 and 0 <= tx < 3:
                lag_t[t, d] = dw_t[ty * 3 + tx]
    arrays = {
        "x": np.asarray(x),
        "qkv_wT": np.asarray(L0_conv_qkv_w)[:, :, 0, 0].T,
        "dw_t": dw_t,
        "lag_t": lag_t,
        "dw_rep": np.broadcast_to(dw_t, (K1, TAPS, QK)),
        "dw_v": dw[QK:],
        "proj_wT": np.asarray(L0_conv_proj_w)[:, :, 0, 0].T,
        "w1T": np.asarray(L1_conv_w1).T,
        "bn": np.stack([np.asarray(a) for a in (L1_conv_gamma, L1_conv_beta, L1_conv_running_mean,
                                                L1_conv_running_var)], 1),
        "w2T": np.asarray(L1_conv_w2).reshape(C, TAPS, RED).transpose(2, 1, 0),
        "b2": np.asarray(L1_conv_b2).reshape(C, TAPS),
        "bias": np.asarray(L1_conv_bias).reshape(C, 1),
        "const": constants(),
        "ends": np.concatenate([np.ones((1, W), np.float32), np.zeros((K1, W), np.float32)]),
    }
    arrays = {f"in_{name}": np.ascontiguousarray(a) for name, a in arrays.items()}
    nc = bacc.Bacc("TRN2", target_bir_lowering=False, num_devices=1)
    args = [nc.dram_tensor(name, a.shape, mybir.dt.from_np(a.dtype), kind="ExternalInput").ap()
            for name, a in arrays.items()]
    out = nc.dram_tensor("out", (B, C, H, W), mybir.dt.float32, kind="ExternalOutput").ap()
    build(nc, *args, out)
    result = run_bass_kernel_spmd(nc, [arrays], core_ids=[0])
    return result.results[0]["out"]
```

```python
from contextlib import ExitStack

import numpy as np

import concourse.bass as bass
from concourse import mybir

B, C, H, W = 8, 96, 256, 256
HEADS = 6
HD = C // HEADS
GN_GROUPS = 32
CPG = C // GN_GROUPS
RED = 24
K1 = C + 1
K2 = K1 + 1
QK = 2 * C
GN_EPS = 1e-5
BN_EPS = 1e-5
NORM_EPS = 1e-12
TAPS = 9

WP = W + 4
WB = W + 2
U = 8
NU = H // U
RING = 16
LAG = 6
LAGS = [(0, dy) for dy in range(3)] + [(dx, dy) for dx in (1, 2) for dy in range(-2, 3)]
NL = len(LAGS)
LAG_W = 5 * K2
V_TAPS = (1, 2, 3, 5, 6, 7, 8)
Y_TAPS = tuple(range(1, TAPS))

CG = 4
BL = 128 // CG
NG = C // CG
NV = TAPS + 2
NP = NV + 2
PAIRS = H // 2
UP = U // 2
EDGES = [(i, n) for i in range(2) for n in range(3)] + [(i, n) for i in (2, 3) for n in range(2)]
EP = (W + 2) // 3

A_ROWS = 16
UK, U_ROWS = 6, 16
U_TURNS = NU // UK
U_AT = [(0, 3), (3, 6), (6, 8), (8, 11), (11, 14), (14, 16)]
D_ROWS = 16
GK, G_ROWS = 8, 48
G_TURNS = NG // GK
G_EACH = G_ROWS // GK
T1_AT = A_ROWS
D_AT = T1_AT + U_TURNS * U_ROWS
T2_AT = D_AT + D_ROWS
assert T2_AT + G_TURNS * G_ROWS == H and NU == U_TURNS * UK + 2 and RING == 2 * U

V_OPS = {3: "rvvrvvvrvv", 2: "rvvvvvrvv"}
Y_OPS = "ryyryryyryryry"
assert all(o.count("r") == n and o.count("v") == len(V_TAPS) for n, o in V_OPS.items())
assert Y_OPS.count("r") == G_EACH and Y_OPS.count("y") == len(Y_TAPS)

Y_PE = Y_TAPS[-3:]

COLS = {}
_at = 0
for _name, _n in (("ident", 128), ("avg_sum", C), ("spread", 128), ("group_of", NG), ("off_head", C),
                  ("inside", 2), ("zero", 256)):
    COLS[_name] = (_at, _at + _n)
    _at += _n
NCONST = _at


def constants():
    t = np.zeros((128, NCONST), np.float32)

    def part(name):
        a, b = COLS[name]
        return t[:, a:b]

    part("ident")[:] = np.eye(128)
    c = np.arange(C)
    part("avg_sum")[:C] = (c[:, None] // CPG == c[None] // CPG) / (CPG * H * W)
    part("spread")[:C] = c[:, None] % CG == np.arange(128)[None] // BL
    part("group_of")[:C] = c[:, None] // CG == np.arange(NG)[None]
    part("off_head")[:C] = np.where(c[:, None] // HD == c[None] // HD, 0.0, -1e30)
    block = np.arange(128) % BL
    part("inside")[:, 0] = block > 0
    part("inside")[:, 1] = block < BL - 1
    return t


PE_ATT = (["means0", "folded", "folded_vT", "folded_v"] + [f"lag_w{j}" for j in range(7)]
          + [f"lag_qk{d}" for d in range(NL)] + [f"ring{j}" for j in range(10)]
          + ["ring_qk", "dots_t", "logits", "attn_proj", "middle"])
DVE_ATT = (["lags0", "squares0", "sums0", "sumsq0", "mean0", "meansq0", "var0", "vareps0", "rstd0", "fold_diag0",
            "fold0", "folded_qk", "ring_taps"]
           + [f"lag_dots{d}" for d in range(NL)]
           + ["dots", "dots_ring", "own", "own_sum", "norm_sq", "norm_inv", "norm_q", "dots_kq", "dots_k",
              "masked", "max", "max_neg", "sum_inv", "attn", "out_w", "middle_tap", "middle_w"])
ACT_ATT = (["lags1", "lags2", "edges", "std0", "folded_vT", "folded_v"] + [f"lag_w{j}" for j in range(7)]
           + [f"ring{j}" for j in range(10)] + ["norm", "exp"])
PE_DYN = ["means1", "hidden", "dynamic", "spread"]
DVE_DYN = ["sums1", "mean1", "meansq1", "var1", "vareps1", "rstd1", "channel1", "pooled", "dyn_b2", "taps1",
           "taps1_res", "col_mean", "col_bias", "columns", "taps_spread", "edge_means"]
ACT_DYN = ["std1", "gate"]


def at(steps, name):
    return steps.index(name) + 1


def build(nc, x, qkv_wT, dw_t, lag_t, dw_rep, dw_v, proj_wT, w1T, bn, w2T, b2, bias, const, ends, out):
    f32 = mybir.dt.float32
    f32r = mybir.dt.float32r
    ALU = mybir.AluOpType
    ACT = mybir.ActivationFunctionType
    AX = mybir.AxisListType.X
    x1_dram = nc.dram_tensor("x1", [B, C * H + 2, W], f32, kind="Internal").ap()
    coef_dram = nc.dram_tensor("coef", [C, NL, 2 * QK], f32, kind="Internal").ap()
    N_PA, N_DA, N_AA = len(PE_ATT), len(DVE_ATT), len(ACT_ATT)
    N_PD, N_DD, N_AD = len(PE_DYN), len(DVE_DYN), len(ACT_DYN)

    with ExitStack() as ctx:
        def sb(name, shape, dt=f32):
            return ctx.enter_context(nc.sbuf_tensor(name, shape, dt))

        def sem(name):
            return ctx.enter_context(nc.semaphore(name))

        xc = [sb(f"lag_x_{n}", [K1, U, WP]) for n in "ab"]
        xt_hi = sb("xt_hi", [128, RING, 4, K2], f32r)
        xt_lo = sb("xt_lo", [128, RING, 4, K2], f32r)
        xp = [sb(f"conv_x_{n}", [K1, U + 1, W]) for n in "abc"]
        vb = [sb(f"v_rows_{n}", [C, U + 2, WB]) for n in "ab"]
        va = sb("v_sum", [128, 2 * U * W])
        v_sum = [va[0:C, i * U * W:(i + 1) * U * W].rearrange("p (r w) -> p r w", w=W) for i in range(2)]
        rows_out = sb("rows_out", [128, U * W])
        lags = rows_out[0:K1, 0:3 * LAG_W].rearrange("p (d a) -> p d a", d=3)
        strips = sb("x1_strips", [128, 2, U + 2, WB])
        xs = [strips[:, j, :, :] for j in range(2)]
        results = sb("results", [128, 2, U, W])
        ys = [results[:, j, :, :] for j in range(2)]
        strips_flat = strips[:, :, :, :].rearrange("p g r w -> p (g r w)")
        results_flat = results[:, :, :, :].rearrange("p g r w -> p (g r w)")
        lag_coef = strips_flat[0:C, 0:NL * 2 * QK].rearrange("p (d a) -> p d a", d=NL)
        lagw = results_flat[0:K1, 0:NL * QK].rearrange("p (d a) -> p d a", d=NL)
        dots_all = lag_coef
        ring_w = va[0:K1, 0:TAPS * QK].rearrange("p (t a) -> p t a", t=TAPS)
        ct = sb("constants", [128, NCONST])
        w_qkvT = sb("w_qkvT", [C, 3 * C])
        w_projT = sb("w_projT", [C, C])
        w_1T = sb("w_1T", [C, RED])
        w_2T = sb("w_2T", [RED, TAPS, C])
        b_2 = sb("b_2", [C, TAPS])
        b_out = sb("b_out", [C, 1])
        v_dw = sb("v_dw", [C, TAPS])
        bn_in = sb("bn_in", [RED, 4])
        bn_sb = sb("bn_scale_shift", [RED, 4])
        taps_qk = sb("taps_qk", [TAPS, QK])
        taps_lag = results_flat[0:TAPS, 0:NL * QK].rearrange("p (d a) -> p d a", d=NL)
        diag = [va[:, i * U * W:i * U * W + len(Y_PE) * 128].rearrange("p (t c) -> p t c", t=len(Y_PE))
                for i in range(2)]
        edge_rows = sb("edge_rows", [K1, 2, WP])
        edge_cols = sb("edge_cols", [K1, 2, H + 2])
        edge_cols_kept = sb("edge_cols_kept", [K1, 2, H + 2])
        mom_turn = sb("moments_turn", [C, 2, UK * UP])
        x1_mom = sb("x1_moments", [C, 2, PAIRS])
        dw_all = sb("dw_all", [K1, TAPS, QK])
        sq0 = sb("sq0", [C, C])
        tap_w = sq0
        st0 = sb("st0", [C, 2])
        gm0 = sb("gm0", [C, 6])
        fold = sb("fold", [C, K1])
        w_fold = sb("w_fold", [K1, QK])
        v_foldT = sb("v_foldT", [K1, C])
        v_fold = sb("v_fold", [C, K1])
        out_w = sb("out_w", [C, C])
        mid_tap = sb("mid_tap", [C, C])
        mid_w = sb("mid_w", [K1, C])
        ring_sb = sb("ring_sb", [128, 2, QK])
        dots = sb("dots", [C, 2 * QK])
        own = sb("own", [C, 2, C])
        nrm = sb("nrm", [C, 10])
        att = sb("att", [C, 5, C])
        st1 = sb("st1", [C, 2])
        gm1 = sb("gm1", [C, 8])
        hid = sb("hid", [RED, 1])
        dyn = sb("dyn", [C, TAPS])
        vec1 = sb("vec1", [C, NV])
        cols1 = sb("cols1", [C, NG, NV])
        par_all = sb("par_all", [128, NG, NP])
        par = sb("par", [128, GK, NP])

        def const_(name, parts):
            a, b = COLS[name]
            return ct[0:parts, a:b]

        def ps(name):
            return ctx.enter_context(nc.psum_tensor(name, [128, 512], f32))

        acc = [ps(f"lag_acc{i}") for i in range(3)]
        bank = [ps(f"bank{i}") for i in range(5)]
        y_banks = (acc + bank[0:1], bank[1:5])
        v_bank, x1_bank = (bank[2], bank[3], bank[4], bank[2]), (bank[3], bank[4], bank[3], bank[4])
        v_bank_last, x1_bank_last = (bank[2], bank[0], bank[1], acc[0]), (bank[3], bank[4], acc[1], acc[2])

        setup_loaded = sem("setup_loaded")
        setup_zeros = sem("setup_zeros")
        setup_pe, setup_dve, setup_act = sem("setup_pe"), sem("setup_dve"), sem("setup_act")
        coef_stored, coef_loaded = sem("coef_stored"), sem("coef_loaded")
        x_loaded = [sem(f"x_loaded_{n}") for n in "ab"]
        edge_rows_loaded = sem("edge_rows_loaded")
        edges_taken = sem("edges_taken")
        row_turned = sem("row_turned")
        row_hi, row_lo = sem("row_hi"), sem("row_lo")
        lags_summed = sem("lags_summed")
        xp_loaded = [sem(f"xp_loaded_{n}") for n in "abc"]
        xp_end_loaded = sem("xp_end_loaded")
        v_ready, v_kept = sem("v_ready"), sem("v_kept")
        v_topped = sem("v_topped")
        v_halo = sem("v_halo")
        v_begun = sem("v_begun")
        v_tap = sem("v_tap")
        tap_w_ready = sem("tap_w_ready")
        x1_ready, x1_copied = sem("x1_ready"), sem("x1_copied")
        x1_summed = sem("x1_summed")
        x1_stored = sem("x1_stored")
        pe_att, dve_att, act_att = sem("pe_att"), sem("dve_att"), sem("act_att")
        pe_dyn, dve_dyn, act_dyn = sem("pe_dyn"), sem("dve_dyn"), sem("act_dyn")
        pads_zeroed = sem("pads_zeroed")
        xs_loaded = [sem(f"xs_loaded_{j}") for j in range(2)]
        par_taken = sem("par_taken")
        xs_centred = sem("xs_centred")
        diag_ready = sem("diag_ready")
        y_products = sem("y_products")
        y_begun = sem("y_begun")
        y_tap = sem("y_tap")
        y_stored = [sem(f"y_stored_{j}") for j in range(2)]

        SETUP_DMAS = 12
        counted_from_first = [v_kept, x1_ready, x1_copied, x1_stored, y_tap]
        FIRST = 1
        FIRST_STORE = 16
        NVT, NYT = len(V_TAPS), len(Y_TAPS)
        NYT_LAST = NYT - len(Y_PE) + UP
        XP_LOADS = [len(range(i, NU, 3)) for i in range(3)]
        VP = PAIRS + 1
        block = ctx.enter_context(nc.Block())

        def pipeline(eng, step):
            step(0, True, False)
            with eng.Fori(1, B) as s:
                step(s, True, True)
            step(B, False, True)

        def rows_only(eng, row):
            with eng.Fori(0, (H - T1_AT) // RING) as k:
                for r in range(RING):
                    row(T1_AT + k * RING, r)

        @block.sync
        def _(sp):
            for dst, src in ((ct[:, :], const), (w_qkvT[:, :], qkv_wT), (w_projT[:, :], proj_wT), (w_1T[:, :], w1T),
                             (w_2T[:, :, :], w2T), (b_2[:, :], b2), (b_out[:, :], bias), (v_dw[:, :], dw_v),
                             (bn_in[:, :], bn), (taps_qk[:, :], dw_t), (taps_lag, lag_t),
                             (dw_all[:, :, :], dw_rep)):
                sp.dma_start(dst, src).then_inc(setup_loaded, 16)
            sp.wait_ge(setup_loaded, 16 * SETUP_DMAS)
            sp.wait_ge(setup_dve, NL)
            sp.dma_start(coef_dram, lag_coef).then_inc(coef_stored, 16)
            sp.wait_ge(coef_stored, 16)
            sp.wait_ge(setup_zeros, 17)

            def step(s, lags_, rest):
                a, b = s, s - 1

                def lag_load(unit, c):
                    if not lags_:
                        return
                    free = a * NU if isinstance(unit, int) and unit == 0 else a * NU + unit - 1
                    sp.wait_ge(row_turned, free * U)
                    sp.wait_ge(edges_taken, free)
                    rows = x[bass.ds(a, 1), :, :, :].rearrange("b c h w -> (b c) h w")
                    sp.dma_start(xc[c % 2][0:C, :, 2:2 + W], rows[:, bass.ds(unit * U, U), :]).then_inc(
                        x_loaded[c % 2], 16)

                def conv_load(unit, c, last=False):
                    i = c % 3
                    through = 0 if isinstance(unit, int) and unit < 3 else (unit - 2) * UP
                    sp.wait_ge(x1_ready, FIRST + b * PAIRS + through)
                    rows = x[bass.ds(b, 1), :, :, :].rearrange("b c h w -> (b c) h w")
                    n = U if last else U + 1
                    if last:
                        sp.dma_start(xp[i][0:C, U, :], ends[1:K1, :]).then_inc(xp_end_loaded, 16)
                        sp.wait_ge(xp_end_loaded, (b + 1) * 16)
                    row = K1 if last else 0
                    sp.dma_start(xp[i][C:K1, U, :], ends[row:row + 1, :]).then_inc(xp_loaded[i], 16)
                    sp.dma_start(xp[i][0:C, 0:n, :], rows[:, bass.ds(unit * U, n), :]).then_inc(
                        xp_loaded[i], 16)

                for u in range(A_ROWS // U):
                    lag_load(u, u)
                if rest:
                    sp.wait_ge(y_tap, FIRST + b * NG * NYT)
                    sp.dma_start(lag_coef, coef_dram).then_inc(coef_loaded, 16)
                    for u in range(2):
                        conv_load(u, u)

                    def turn(k, last=False):
                        for c in range(UK):
                            if c % 3 == 0:
                                lag_load(T1_AT // U + k * 2 + c // 3, c // 3)
                            conv_load(k * UK + c + 2, c + 2, last and c == UK - 1)

                    with sp.Fori(0, U_TURNS - 1) as k:
                        turn(k)
                    turn(U_TURNS - 1, last=True)
                if lags_:
                    first = (D_AT if rest else T1_AT) // U
                    for u in range(2):
                        lag_load(first + u, u)
                    for i in range(2):
                        if rest:
                            sp.wait_ge(pe_att, s * N_PA)
                        sp.dma_start(edge_rows[0:C, i, 2:2 + W],
                                     x[bass.ds(a, 1), :, i * (H - 1), :].rearrange("b c w -> (b c) w")).then_inc(
                                         edge_rows_loaded, 16)
                    with sp.Fori(0, (NU - first) // 2 - 1) as k:
                        for u in range(2):
                            lag_load(first + 2 + k * 2 + u, u)

            pipeline(sp, step)

        @block.gpsimd
        def _(pool):
            for n, semaphore in enumerate(counted_from_first):
                nc.gpsimd.memset(par[:, 0, n:n + 1], 0.0).then_inc(semaphore, FIRST)
            n = 0
            for borders in (xc[0][:, :, :], xc[1][:, :, :], xp[0][:, :, :], xp[1][:, :, :], xp[2][:, :, :],
                            edge_cols[:, :, :], edge_rows[:, :, :], vb[0][:, :, :], vb[1][:, :, :], xt_hi[:, :, :, K1:K2].bitcast(f32),
                            xt_lo[:, :, :, K1:K2].bitcast(f32)):
                nc.gpsimd.memset(borders, 0.0).then_inc(setup_zeros, 1)
                n += 1
                pool.wait_ge(setup_zeros, n)
            for ones in (xc[0][C:K1, :, 2:2 + W], xc[1][C:K1, :, 2:2 + W], edge_rows[C:K1, :, 2:2 + W],
                         xp[0][C:K1, :, :], xp[1][C:K1, :, :], xp[2][C:K1, :, :]):
                nc.gpsimd.memset(ones, 1.0).then_inc(setup_zeros, 1)
                n += 1
                pool.wait_ge(setup_zeros, n)
            pool.wait_ge(setup_loaded, 16 * SETUP_DMAS)
            for j, r in enumerate((0, C * H + 1)):
                pool.dma_start(x1_dram[:, r, :], const_("zero", B)).then_inc(y_stored[j], FIRST_STORE)
            for j in range(2):
                pool.wait_ge(y_stored[j], FIRST_STORE)

            def step(s, lags_, rest):
                if not rest:
                    return
                b = s - 1
                pool.wait_ge(dve_att, b * N_DA + at(DVE_ATT, "dots_ring"))
                for column in (0, WB - 1):
                    zeros = const_("zero", 128)[:, 0:2 * (U + 2)].rearrange("p (g r) -> p g r", g=2)
                    nc.gpsimd.tensor_tensor(strips[:, :, :, column], zeros, zeros, ALU.add).then_inc(pads_zeroed, 1)
                pool.wait_ge(pads_zeroed, s * 2)
                pool.wait_ge(x1_stored, FIRST + (b + 1) * NU * 16)

                def load(group, j):
                    at_row = b * ((C * H + 2) * W) + group * (CG * H * W)
                    pool.dma_start(xs[j][:, :, 1:1 + W], bass.AP(x1_dram.tensor, at_row,
                                                                 [[U * W, 128], [W, U + 2], [1, W]])).then_inc(
                                                                     xs_loaded[j], 16)

                def store(group, j, load_next):
                    pool.wait_ge(y_tap, FIRST + (b * NG * NYT + (group + 1) * (NYT if lags_ else NYT_LAST)))
                    if load_next:
                        load(group + 2, j)
                    at_row = b * (C * H * W) + group * (CG * H * W)
                    pool.dma_start(bass.AP(out.tensor, at_row, [[U * W, 128], [1, U * W]]),
                                   ys[j].rearrange("p r w -> p (r w)")).then_inc(y_stored[j], 16)

                for j in range(2):
                    load(j, j)
                with pool.Fori(0, NG // 2 - 1) as k:
                    for j in range(2):
                        store(k * 2 + j, j, True)
                for j in range(2):
                    store(NG - 2 + j, j, False)

            pipeline(pool, step)
            for j in range(2):
                pool.wait_ge(y_stored[j], FIRST_STORE + 16 * (NG // 2) * B)

        @block.tensor
        def _(pe):
            ident = const_("ident", K1)[:, 0:K1]
            ident_c = const_("ident", C)[:, 0:C]
            pe.wait_ge(setup_loaded, 16 * SETUP_DMAS)
            for d in range(NL):
                if d >= 5:
                    pe.wait_ge(setup_dve, d - 4)
                for half in range(2):
                    ins = nc.tensor.matmul(bank[d % 5][0:C, half * QK:(half + 1) * QK],
                                           taps_qk[:, half * C:(half + 1) * C], taps_lag[:, d, :],
                                           start=True, stop=True)
                ins.then_inc(setup_pe, 1)
            pe.wait_ge(setup_zeros, 17)
            pe.wait_ge(setup_dve, NL)

            def step(s, lags_, rest):
                a, b = s, s - 1

                def turn_row(base, r, first):
                    i = r // U % 2
                    if r % U == 0:
                        pe.wait_ge(x_loaded[i], (a * NU // 2 + base // RING + r // RING + 1) * 16
                                   if isinstance(base, int) and isinstance(a, int)
                                   else a * H + base + r // RING * 16 + 16)
                    if not (first and r < 2):
                        pe.wait_ge(row_lo, a * H + base + r - 1)
                    for p in range(4):
                        ins = nc.tensor.transpose(bank[r % 2][:, p * K2:p * K2 + K1],
                                                  xc[i][:, r % U, 2 + p:2 + p + W - 1:2], ident)
                    ins.then_inc(row_turned, 1)

                def lag_row(r, lo, hi):
                    for p in range(2):
                        for dx in range(3):
                            first, base = (max(lo, 0), 0) if dx == 0 else (lo, -2)
                            for left, right in ((xt_hi, xt_hi), (xt_hi, xt_lo), (xt_lo, xt_hi)):
                                q = first
                                while q <= hi:
                                    slot = (r + q) % RING
                                    n = min(hi - q + 1, RING - slot)
                                    ins = nc.tensor.matmul(
                                        acc[dx][0:K1, (q - base) * K2:(q - base + n) * K2],
                                        left[:, r % RING, p, 0:K1], right[:, slot:slot + n, p + dx, :],
                                        start=False, stop=False, skip_group_check=True)
                                    q += n
                    return ins

                def row(base, r):
                    if not lags_:
                        return
                    first = isinstance(base, int) and base == 0
                    turn_row(base, r, first)
                    if not first:
                        pe.wait_ge(row_lo, a * H + base + r - LAG + 3)
                        lag_row(r + RING - LAG, -2, 2)
                    elif r >= LAG:
                        pe.wait_ge(row_lo, a * H + r - LAG + 3)
                        lag_row(r - LAG, -min(r - LAG, 2), 2)

                v_banks = v_bank if lags_ else v_bank_last

                def v_pairs(k, c):
                    unit, i = k * UK + c, c % 3
                    pe.wait_ge(xp_loaded[i], b * XP_LOADS[i] * 32 + (k * (UK // 3) + c // 3 + 1) * 32)
                    for p in range(UP):
                        first = isinstance(unit, int) and unit == 0
                        if p == 0:
                            pe.wait_ge(v_kept, FIRST + (b * VP if first else b * VP + 1 + unit * UP))
                        elif lags_ and p < UP - 1:
                            pe.wait_ge(x1_copied, FIRST + (b * PAIRS if first else b * PAIRS + (unit - 1) * UP))
                            if first and p == UP - 2:
                                pe.wait_ge(v_kept, FIRST + b * VP + 1)
                        elif lags_:
                            pe.wait_ge(v_kept, FIRST + b * VP + 1 + unit * UP + 1)
                        nc.tensor.matmul(v_banks[p][0:C, :], v_foldT[:, :], xp[i][:, 1 + 2 * p:3 + 2 * p, :],
                                         start=True, stop=True).then_inc(v_ready, 1)

                def x1_pairs(unit, c):
                    for p in range(UP):
                        if p < 2:
                            pe.wait_ge(v_kept, FIRST + (b * VP + 1 + (unit + 1) * UP + (0 if c == NU - 1 else p + 2)))
                        if p == 0:
                            pe.wait_ge(x1_copied, FIRST + b * PAIRS + unit * UP)
                        elif p >= 2:
                            pe.wait_ge(x1_copied, FIRST + b * PAIRS + unit * UP + p - 1)
                        o = x1_bank[p][0:C, :]
                        nc.tensor.matmul(o, mid_w[:, :], xp[c % 3][:, 2 * p:2 * p + 2, :], start=True, stop=False)
                        if p == 0:
                            pe.wait_ge(v_tap, (b * NU + unit + 1) * NVT)
                        nc.tensor.matmul(o, out_w[:, :], v_sum[c % 2][:, 2 * p:2 * p + 2, :], start=False,
                                         stop=True).then_inc(x1_ready, 1)

                def x1_pairs_last(unit, c):
                    dy, dx = V_TAPS[-1] // 3, V_TAPS[-1] % 3
                    pe.wait_ge(v_begun, b * NU + unit + 1)
                    for p in range(UP):
                        pe.wait_ge(x1_copied, FIRST + b * PAIRS + (unit - 1) * UP + p + 1)
                        o = x1_bank_last[p][0:C, :]
                        nc.tensor.matmul(o, mid_w[:, :], xp[c % 3][:, 2 * p:2 * p + 2, :], start=True, stop=False)
                        nc.tensor.matmul(o, tap_w[:, :], vb[c % 2][:, 2 * p + dy:2 * p + dy + 2, dx:dx + W],
                                         start=False, stop=False)
                    pe.wait_ge(v_tap, b * NU * NVT + (unit + 1) * (NVT - 1))
                    for p in range(UP):
                        nc.tensor.matmul(x1_bank_last[p][0:C, :], out_w[:, :], v_sum[c % 2][:, 2 * p:2 * p + 2, :],
                                         start=False, stop=True).then_inc(x1_ready, 1)

                def y_products_of(group, j):
                    pe.wait_ge(diag_ready, (group + j + 1) * len(Y_PE))
                    pe.wait_ge(y_tap, FIRST + b * NG * NYT + (group + j - 1) * NYT_LAST)
                    for q in range(UP):
                        for i, t in enumerate(Y_PE):
                            dy, dx = t // 3, t % 3
                            ins = nc.tensor.matmul(y_banks[j][q][:, :], diag[j][:, i, :],
                                                   xs[j][:, 2 * q + dy:2 * q + dy + 2, dx:dx + W],
                                                   start=(i == 0), stop=(i == len(Y_PE) - 1))
                        ins.then_inc(y_products, 1)

                def zero_lags():
                    for dx in range(3):
                        n = (3 if dx == 0 else 5) * K2
                        nc.tensor.matmul(acc[dx][0:K1, 0:n], const_("zero", 128)[:, 0:K1], ct[:, 0:n],
                                         start=True, stop=False, skip_group_check=True)

                if not rest:
                    zero_lags()
                    for r in range(A_ROWS):
                        row(0, r)
                    rows_only(pe, row)
                else:
                    attention(b, zero_lags if lags_ else None, lambda r: row(0, r))
                    pe.wait_ge(dve_att, s * N_DA)
                    pe.wait_ge(xp_loaded[0], b * XP_LOADS[0] * 32 + 32)
                    nc.tensor.matmul(x1_bank[1][0:C, 0:W], v_foldT[:, :], xp[0][:, 0, :], start=True,
                                     stop=True).then_inc(v_ready, 1)
                    v_pairs(0, 0)
                    if not lags_:
                        pe.wait_ge(tap_w_ready, 1)
                    for r in (14, 15):
                        row(0, r)
                    with pe.Fori(0, U_TURNS) as k:
                        for c in range(UK):
                            v_pairs(k, c + 1)
                            r0, r1 = U_AT[c]
                            for r in range(r0, r1 - 1):
                                row(T1_AT + k * U_ROWS, r)
                            (x1_pairs if lags_ else x1_pairs_last)(k * UK + c, c)
                            row(T1_AT + k * U_ROWS, r1 - 1)
                    dynamic(b, v_pairs, x1_pairs if lags_ else x1_pairs_last, lambda r: row(D_AT, r))
                    if lags_:
                        with pe.Fori(0, G_TURNS) as k:
                            for r in range(G_ROWS):
                                row(T2_AT + k * G_ROWS, r)
                    else:
                        pe.wait_ge(dve_dyn, s * N_DD)
                        y_products_of(0, 0)
                        y_products_of(0, 1)
                        with pe.Fori(0, NG // 2 - 1) as k:
                            for j in range(2):
                                y_products_of(k * 2 + 2, j)
                if lags_:
                    for q in range(H - LAG, H):
                        pe.wait_ge(row_lo, a * H + min(q + 3, H))
                        ins = lag_row(q % RING, -2, min(2, H - 1 - q))
                    ins.then_inc(lags_summed, 1)

            def dynamic(b, v_pairs, x1_pairs, row):
                def step(ins):
                    ins.then_inc(pe_dyn, 1)

                def rows(first, last):
                    for r in range(first, last):
                        row(r)

                def dve_d(name):
                    pe.wait_ge(dve_dyn, b * N_DD + at(DVE_DYN, name))

                small = bank[3]
                v_pairs(0, NU - 1)
                rows(0, 2)
                x1_pairs(NU - 2, NU - 2)
                rows(2, 6)
                x1_pairs(NU - 1, NU - 1)
                rows(6, 8)
                dve_d("sums1")
                step(nc.tensor.matmul(small[0:C, 0:2], const_("avg_sum", C), st1[:, :], start=True, stop=True))
                rows(8, 11)
                dve_d("pooled")
                step(nc.tensor.matmul(small[0:RED, 0:1], w_1T[:, :], gm1[:, 6:7], start=True, stop=True))
                rows(11, 12)
                pe.wait_ge(act_dyn, b * N_AD + at(ACT_DYN, "gate"))
                for t in range(TAPS):
                    ins = nc.tensor.matmul(small[0:C, t:t + 1], w_2T[:, t, :], hid[:, :], start=True, stop=True)
                step(ins)
                rows(12, 14)
                dve_d("columns")
                step(nc.tensor.matmul(small[:, 0:NG * NV], const_("spread", C), cols1[:, :, :], start=True, stop=True))
                rows(14, 16)

            def attention(b, zero_lags, row):
                def step(ins):
                    ins.then_inc(pe_att, 1)

                def rows(first, last):
                    for r in range(first, last):
                        row(r)

                def dve(name):
                    pe.wait_ge(dve_att, b * N_DA + at(DVE_ATT, name))

                def act(name):
                    pe.wait_ge(act_att, b * N_AA + at(ACT_ATT, name))

                small = bank[4]
                rows(0, 2)
                if zero_lags is not None:
                    dve("lags0")
                    act("lags2")
                    zero_lags()
                dve("sumsq0")
                step(nc.tensor.matmul(small[0:C, 0:2], const_("avg_sum", C), st0[:, :], start=True, stop=True))
                rows(2, 4)
                dve("fold0")
                step(nc.tensor.matmul(bank[2][0:K1, 0:QK], fold[:, :], w_qkvT[:, 0:QK], start=True, stop=True))
                step(nc.tensor.matmul(bank[3][0:K1, 0:C], fold[:, :], w_qkvT[:, QK:3 * C], start=True, stop=True))
                step(nc.tensor.matmul(bank[3][0:C, C:C + K1], w_qkvT[:, QK:3 * C], fold[:, :], start=True, stop=True))
                rows(4, 6)
                act("folded_v")
                dve("folded_qk")
                for j in range(7):
                    if j >= 2:
                        act(f"lag_w{j - 2}")
                    for d in range(2 * j, min(2 * j + 2, NL)):
                        dx, i = (0, d) if d < 3 else (1 + (d - 3) // 5, (d - 3) % 5)
                        ins = nc.tensor.matmul(bank[2 + j % 2][0:K1, (d % 2) * QK:(d % 2 + 1) * QK],
                                               lags[:, dx, i * K2:i * K2 + K1], w_fold[:, :], start=True, stop=True)
                    step(ins)
                rows(6, 7)
                act("lag_w6")
                for d in range(NL):
                    if d >= 3:
                        dve(f"lag_dots{d - 3}")
                    for half in range(2):
                        ins = nc.tensor.matmul(bank[2 + d % 3][0:C, half * QK:(half + 1) * QK],
                                               lagw[:, d, half * C:(half + 1) * C], w_fold[:, :],
                                               start=True, stop=True)
                    step(ins)
                rows(7, 9)
                dve("ring_taps")
                dve(f"lag_dots{NL - 1}")
                pe.wait_ge(edge_rows_loaded, (b + 1) * 32)

                def ring_dots(j):
                    act(f"ring{j}")
                    side, _ = EDGES[j]
                    n = EP if side < 2 else 128
                    for half in range(2):
                        ins = nc.tensor.matmul(bank[4][0:C, half * QK:(half + 1) * QK],
                                               ring_sb[0:n, j % 2, half * C:(half + 1) * C], ring_sb[0:n, j % 2, :],
                                               start=(j == 0 and half == 0), stop=(j == len(EDGES) - 1),
                                               skip_group_check=True)
                    return ins

                for j, (side, piece) in enumerate(EDGES):
                    n = EP if side < 2 else 128
                    if j >= 2:
                        act(f"ring{j - 2}")
                    if j == 5:
                        rows(9, 10)
                    for t in range(3):
                        if side < 2:
                            src = edge_rows[:, side, piece * EP + t:piece * EP + t + EP]
                            tap = (1 - side) * 6 + t
                        else:
                            src = edge_cols_kept[:, side - 2, piece * 128 + t:piece * 128 + t + 128]
                            tap = 3 * t + (3 - side) * 2
                        ins = nc.tensor.matmul(bank[2 + j % 2][0:n, 0:QK], src, ring_w[:, tap, :],
                                               start=(t == 0), stop=(t == 2))
                    step(ins)
                    if j >= 1:
                        ring_dots(j - 1)
                step(ring_dots(len(EDGES) - 1))
                small = bank[3]
                rows(10, 11)
                dve("dots_ring")
                step(nc.tensor.transpose(small[0:C, 0:C], dots[:, C:QK], ident_c))
                rows(11, 12)
                dve("dots_k")
                step(nc.tensor.transpose(small[0:C, 0:C], att[:, 1, :], ident_c))
                rows(12, 14)
                dve("attn")
                step(nc.tensor.matmul(small[0:C, 0:C], att[:, 4, :], w_projT[:, :], start=True, stop=True))
                dve("middle_tap")
                step(nc.tensor.matmul(bank[2][0:K1, 0:C], v_fold[:, :], mid_tap[:, :], start=True, stop=True))

            pipeline(pe, step)

        @block.vector
        def _(dve):
            dve.wait_ge(setup_loaded, 16 * SETUP_DMAS)
            for d in range(NL):
                dve.wait_ge(setup_pe, d + 1)
                nc.vector.tensor_scalar(lag_coef[:, d, :], bank[d % 5][0:C, 0:2 * QK], 0.5 if d == 0 else 1.0, None,
                                        ALU.mult).then_inc(setup_dve, 1)
            nc.vector.tensor_scalar(bn_sb[:, 2:3], bn_in[:, 3:4], BN_EPS, None, ALU.add).then_inc(setup_dve, 1)
            dve.wait_ge(setup_act, 1)
            nc.vector.reciprocal(bn_sb[:, 2:3], bn_sb[:, 3:4]).then_inc(setup_dve, 1)
            dve.wait_ge(setup_dve, NL + 2)
            nc.vector.tensor_tensor(bn_sb[:, 0:1], bn_sb[:, 2:3], bn_in[:, 0:1], ALU.mult).then_inc(setup_dve, 1)
            dve.wait_ge(setup_dve, NL + 3)
            nc.vector.tensor_tensor(bn_sb[:, 3:4], bn_sb[:, 0:1], bn_in[:, 2:3], ALU.mult).then_inc(setup_dve, 1)
            dve.wait_ge(setup_dve, NL + 4)
            nc.vector.tensor_tensor(bn_sb[:, 1:2], bn_in[:, 1:2], bn_sb[:, 3:4], ALU.subtract).then_inc(setup_dve, 1)
            dve.wait_ge(setup_dve, NL + 5)
            ident_c = const_("ident", C)[:, 0:C]

            def step(s, lags_, rest):
                a, b = s, s - 1

                def low_half(base, r):
                    if not lags_:
                        return
                    dve.wait_ge(row_hi, a * H + base + r + 1)
                    turned = bank[r % 2][:, 0:4 * K2].rearrange("p (s c) -> p s c", c=K2)[:, :, 0:K1]
                    nc.vector.tensor_tensor(xt_lo[:, r % RING, :, 0:K1], turned,
                                            xt_hi[:, r % RING, :, 0:K1].bitcast(f32), ALU.subtract).then_inc(row_lo, 1)

                nv = NVT if lags_ else NVT - 1

                def v_op(unit, c, n):
                    if n == 0:
                        dve.wait_ge(v_begun, b * NU + unit + 1)
                    else:
                        dve.wait_ge(v_tap, b * NU * NVT + unit * nv + n)
                    t = V_TAPS[n]
                    dy, dx = t // 3, t % 3
                    nc.vector.scalar_tensor_tensor(v_sum[c % 2], vb[c % 2][:, dy:dy + U, dx:dx + W], v_dw[:, t:t + 1],
                                                   v_sum[c % 2], ALU.mult, ALU.add).then_inc(v_tap, 1)

                ny = NYT if lags_ else NYT_LAST

                def y_op(group, j, n):
                    taps = NYT if lags_ else NYT - len(Y_PE)
                    if n == 0:
                        dve.wait_ge(y_begun, b * NG + group + 1)
                    elif n <= taps:
                        dve.wait_ge(y_tap, FIRST + b * NG * NYT + group * ny + n)
                    if n < taps:
                        t = Y_TAPS[n]
                        dy, dx = t // 3, t % 3
                        nc.vector.scalar_tensor_tensor(ys[j % 2], xs[j % 2][:, dy:dy + U, dx:dx + W], par[:, j, t:t + 1],
                                                       ys[j % 2], ALU.mult, ALU.add).then_inc(y_tap, 1)
                    else:
                        q = n - taps
                        dve.wait_ge(y_products, group * UP + q + 1)
                        part = ys[j % 2][:, 2 * q:2 * q + 2, :].rearrange("p r w -> p (r w)")
                        nc.vector.tensor_tensor(part, part, y_banks[j % 2][q][:, :], ALU.add).then_inc(y_tap, 1)

                def v_unit(unit, c, base, first, last, ops=None):
                    n, r = 0, first
                    for op in ops or V_OPS[last - first]:
                        if op == "r":
                            low_half(base, r)
                            r += 1
                        elif n < nv:
                            v_op(unit, c, n)
                            n += 1

                if not rest:
                    for r in range(A_ROWS):
                        low_half(0, r)
                    rows_only(dve, low_half)
                    return
                attention(b, lambda r: low_half(0, r))
                if not lags_:
                    t = V_TAPS[-1]
                    nc.vector.tensor_scalar(tap_w[:, :], out_w[:, :], v_dw[:, t:t + 1], None, ALU.mult).then_inc(
                        tap_w_ready, 1)
                v_unit(0, 0, 0, 14, 16, "rvrvvvvvv")
                with dve.Fori(0, U_TURNS) as k:
                    for c in range(UK):
                        v_unit(k * UK + c + 1, c + 1, T1_AT + k * U_ROWS, *U_AT[c])
                v_unit(NU - 1, NU - 1, D_AT, 0, 3)
                dynamic(b, lambda r: low_half(D_AT, r))

                def parameters(k, first, last):
                    nc.vector.tensor_scalar(par[:, first:last, :], par_all[:, bass.ds(k * GK + first, last - first), :],
                                            1.0, None, ALU.mult).then_inc(par_taken, 1)

                def groups(k, last=False):
                    dve.wait_ge(y_tap, FIRST + b * NG * NYT + k * GK * ny)
                    parameters(k, 1, GK)
                    for j in range(GK):
                        if j == GK - 1 and not last:
                            dve.wait_ge(y_tap, FIRST + b * NG * NYT + (k * GK + j) * ny)
                            parameters(k + 1, 0, 1)
                        n, r = 0, j * G_EACH
                        for op in Y_OPS:
                            if op == "r":
                                low_half(T2_AT + k * G_ROWS, r)
                                r += 1
                            else:
                                y_op(k * GK + j, j, n)
                                n += 1
                        while n < ny:
                            y_op(k * GK + j, j, n)
                            n += 1

                dve.wait_ge(y_tap, FIRST + b * NG * NYT)
                parameters(0, 0, 1)
                with dve.Fori(0, G_TURNS - 1) as k:
                    groups(k)
                groups(G_TURNS - 1, last=True)

            def group_scale(gm, mom, tag, step, after, pe, act, between=None):
                pe("means" + tag)
                step(nc.vector.tensor_copy(gm[:, 0:1], mom[:, 0:1]))
                after("mean" + tag)
                step(nc.vector.tensor_tensor(gm[:, 1:2], gm[:, 0:1], gm[:, 0:1], ALU.mult))
                after("meansq" + tag)
                step(nc.vector.tensor_tensor(gm[:, 2:3], mom[:, 1:2], gm[:, 1:2], ALU.subtract))
                after("var" + tag)
                step(nc.vector.tensor_scalar(gm[:, 3:4], gm[:, 2:3], 0.0, GN_EPS, ALU.max, ALU.add))
                if between is not None:
                    between()
                act("std" + tag)
                step(nc.vector.reciprocal(gm[:, 5:6], gm[:, 4:5]))

            def dynamic(b, row):
                def rows(first, last):
                    for r in range(first, last):
                        row(r)

                def after(name):
                    dve.wait_ge(dve_dyn, b * N_DD + at(DVE_DYN, name))

                def pe(name):
                    dve.wait_ge(pe_dyn, b * N_PD + at(PE_DYN, name))

                def act(name):
                    dve.wait_ge(act_dyn, b * N_AD + at(ACT_DYN, name))

                def step(ins):
                    ins.then_inc(dve_dyn, 1)

                small = bank[3]
                rows(3, 8)
                dve.wait_ge(x1_summed, (b + 1) * U_TURNS)
                dve.wait_ge(x1_copied, FIRST + (b + 1) * PAIRS)
                step(nc.vector.reduce_sum(st1[:, :], x1_mom[:, :, :], AX))
                group_scale(gm1, small[0:C, 0:2], "1", step, after, pe, act)
                step(nc.vector.tensor_scalar(gm1[:, 7:8], st1[:, 0:1], 1.0 / (H * W), gm1[:, 0:1],
                                             ALU.mult, ALU.subtract))
                after("channel1")
                step(nc.vector.tensor_tensor(gm1[:, 6:7], gm1[:, 7:8], gm1[:, 5:6], ALU.mult))
                rows(8, 12)
                pe("dynamic")
                step(nc.vector.tensor_tensor(dyn[:, :], small[0:C, 0:TAPS], b_2[:, :], ALU.add))
                after("dyn_b2")
                step(nc.vector.tensor_scalar(vec1[:, 0:TAPS], dyn[:, :], gm1[:, 5:6], None, ALU.mult))
                after("taps1")
                step(nc.vector.tensor_scalar(vec1[:, 4:5], vec1[:, 4:5], 1.0, None, ALU.add))
                step(nc.vector.tensor_scalar(vec1[:, TAPS:TAPS + 1], gm1[:, 0:1], -1.0, None, ALU.mult))
                step(nc.vector.tensor_tensor(vec1[:, TAPS + 1:NV], gm1[:, 0:1], b_out[:, :], ALU.add))
                after("col_bias")
                step(nc.vector.tensor_tensor(cols1[:, :, :], const_("group_of", C).unsqueeze(2).to_broadcast([C, NG, NV]),
                                             vec1[:, :].unsqueeze(1).to_broadcast([C, NG, NV]), ALU.mult))
                rows(12, 14)
                pe("spread")
                step(nc.vector.tensor_copy(par_all[:, :, 0:NV],
                                           small[:, 0:NG * NV].rearrange("p (g n) -> p g n", n=NV)))
                after("taps_spread")
                step(nc.vector.tensor_tensor(par_all[:, :, NV:NP],
                                             par_all[:, :, TAPS:TAPS + 1].to_broadcast([128, NG, 2]),
                                             const_("inside", 128).unsqueeze(1).to_broadcast([128, NG, 2]), ALU.mult))
                after("edge_means")
                rows(14, 16)

            def attention(b, row):
                def rows(first, last):
                    for r in range(first, last):
                        row(r)

                small = bank[4]

                def after(name):
                    dve.wait_ge(dve_att, b * N_DA + at(DVE_ATT, name))

                def pe(name):
                    dve.wait_ge(pe_att, b * N_PA + at(PE_ATT, name))

                def act(name):
                    dve.wait_ge(act_att, b * N_AA + at(ACT_ATT, name))

                def step(ins):
                    ins.then_inc(dve_att, 1)

                dve.wait_ge(lags_summed, b + 1)
                dve.wait_ge(x1_stored, FIRST + b * NU * 16)
                step(nc.vector.tensor_copy(lags[:, 0, 0:3 * K2], acc[0][0:K1, 0:3 * K2]))
                after("lags0")
                step(nc.vector.tensor_tensor(sq0[:, :], lags[0:C, 0, 0:C], ident_c, ALU.mult))
                step(nc.vector.tensor_copy(st0[:, 0:1], lags[0:C, 0, C:K1]))
                after("squares0")
                step(nc.vector.reduce_sum(st0[:, 1:2], sq0[:, :], AX))
                group_scale(gm0, small[0:C, 0:2], "0", step, after, pe, act, lambda: rows(0, 2))
                after("rstd0")
                step(nc.vector.tensor_scalar(fold[:, 0:C], ident_c, gm0[:, 5:6], None, ALU.mult))
                step(nc.vector.tensor_scalar(fold[:, C:K1], gm0[:, 0:1], gm0[:, 5:6], -1.0, ALU.mult, ALU.mult))
                rows(2, 4)
                pe("folded")
                step(nc.vector.tensor_copy(w_fold[:, :], bank[2][0:K1, 0:QK]))
                rows(4, 6)
                after("folded_qk")
                step(nc.vector.tensor_tensor(ring_w, w_fold[:, :].unsqueeze(1).to_broadcast([K1, TAPS, QK]),
                                             dw_all[:, :, :], ALU.mult))
                dve.wait_ge(coef_loaded, (b + 1) * 16)
                for d in range(NL):
                    pe(f"lag_qk{d}")
                    step(nc.vector.tensor_tensor(dots_all[:, d, :], bank[2 + d % 3][0:C, 0:2 * QK], lag_coef[:, d, :],
                                                 ALU.mult))
                rows(6, 7)
                after(f"lag_dots{NL - 1}")
                step(nc.vector.reduce_sum(dots[:, :], dots_all.rearrange("p d a -> p a d"), AX))
                rows(7, 10)
                pe("ring_qk")
                after("dots")
                step(nc.vector.scalar_tensor_tensor(dots[:, :], bank[4][0:C, 0:2 * QK], -0.5, dots[:, :],
                                                    ALU.mult, ALU.add))
                after("dots_ring")
                own_in = dots[:, :].rearrange("p (a c) -> p a c", c=C)[:, 0:4:3, :]
                step(nc.vector.tensor_tensor(own[:, :, :], own_in, ident_c.unsqueeze(1).to_broadcast([C, 2, C]),
                                             ALU.mult))
                after("own")
                step(nc.vector.reduce_sum(nrm[:, 0:2], own[:, :, :], AX))
                after("own_sum")
                step(nc.vector.tensor_scalar(nrm[:, 2:4], nrm[:, 0:2], 2.0, NORM_EPS ** 2, ALU.mult, ALU.max))
                rows(10, 11)
                act("norm")
                step(nc.vector.reciprocal(nrm[:, 6:8], nrm[:, 4:6]))
                after("norm_inv")
                step(nc.vector.tensor_scalar(nrm[:, 8:9], nrm[:, 6:7], HD ** -0.5, None, ALU.mult))
                pe("dots_t")
                step(nc.vector.tensor_tensor(att[:, 0, :], bank[3][0:C, 0:C], dots[:, QK:QK + C], ALU.add))
                after("dots_kq")
                step(nc.vector.tensor_scalar(att[:, 1, :], att[:, 0, :], nrm[:, 7:8], None, ALU.mult))
                rows(11, 12)
                pe("logits")
                step(nc.vector.scalar_tensor_tensor(att[:, 2, :], bank[3][0:C, 0:C], nrm[:, 8:9],
                                                    const_("off_head", C), ALU.mult, ALU.add))
                after("masked")
                step(nc.vector.reduce_max(nrm[:, 9:10], att[:, 2, :], AX))
                after("max")
                step(nc.vector.tensor_scalar(nrm[:, 0:1], nrm[:, 9:10], -1.0, None, ALU.mult))
                rows(12, 13)
                act("exp")
                step(nc.vector.reciprocal(nrm[:, 2:3], nrm[:, 1:2]))
                after("sum_inv")
                step(nc.vector.tensor_scalar(att[:, 4, :], att[:, 3, :], nrm[:, 2:3], None, ALU.mult))
                rows(13, 14)
                pe("attn_proj")
                step(nc.vector.tensor_copy(out_w[:, :], bank[3][0:C, 0:C]))
                after("out_w")
                step(nc.vector.tensor_scalar(mid_tap[:, :], out_w[:, :], v_dw[:, 4:5], None, ALU.mult))
                pe("middle")
                step(nc.vector.tensor_tensor(mid_w[:, :], bank[2][0:K1, 0:C], const_("ident", K1)[:, 0:C], ALU.add))

            pipeline(dve, step)

        @block.scalar
        def _(eng):
            eng.wait_ge(setup_dve, NL + 1)
            nc.scalar.activation(bn_sb[:, 3:4], bn_sb[:, 2:3], ACT.Sqrt).then_inc(setup_act, 1)

            def copy(dst, src, **more):
                return nc.scalar.activation(dst, src, ACT.Copy, **more)

            def step(s, lags_, rest):
                a, b = s, s - 1

                def high_half(base, r):
                    if not lags_:
                        return
                    eng.wait_ge(row_turned, a * H + base + r + 1)
                    turned = bank[r % 2][:, 0:4 * K2].rearrange("p (s c) -> p s c", c=K2)[:, :, 0:K1]
                    copy(xt_hi[:, r % RING, :, 0:K1], turned).then_inc(row_hi, 1)
                    if r % U == 0:
                        copy(edge_cols[:, :, bass.ds(1 + base + r, U)],
                             xc[r // U % 2][:, :, 2:2 + W:W - 1].rearrange("p r e -> p e r")).then_inc(edges_taken, 1)

                def v_rows(unit, c):
                    for p in range(UP):
                        eng.wait_ge(v_ready, b * VP + 1 + unit * UP + p + 1)
                        if p == 0:
                            eng.wait_ge(v_kept, FIRST + b * VP + 1 + unit * UP)
                            copy(vb[c % 2][:, 0:2, 1:1 + W],
                                 vb[(c + 1) % 2][:, U:U + 2, 1:1 + W]).then_inc(v_halo, 1)
                        src = (v_bank if lags_ else v_bank_last)[p][0:C, :].rearrange("p (r w) -> p r w", w=W)
                        copy(vb[c % 2][:, 2 + 2 * p:4 + 2 * p, 1:1 + W], src).then_inc(v_kept, 1)
                    eng.wait_ge(v_kept, FIRST + b * VP + 1 + (unit + 1) * UP)
                    eng.wait_ge(v_halo, b * NU + unit + 1)
                    nc.scalar.activation(v_sum[c % 2], vb[c % 2][:, 0:U, 0:W], ACT.Identity,
                                         scale=v_dw[:, 0:1]).then_inc(v_begun, 1)

                def x1_rows(unit, mom, m):
                    eng.wait_ge(x1_stored, FIRST + (b * NU + unit) * 16)
                    for p in range(UP):
                        eng.wait_ge(x1_ready, FIRST + b * PAIRS + unit * UP + p + 1)
                        src = (x1_bank if lags_ else x1_bank_last)[p][0:C, :]
                        copy(rows_out[0:C, 2 * p * W:(2 * p + 2) * W], src, accum_out=mom[:, 0, m + p:m + p + 1])
                        nc.scalar.activation(src, src, ACT.Square, accum_out=mom[:, 1, m + p:m + p + 1]).then_inc(
                            x1_copied, 1)
                    eng.wait_ge(x1_copied, FIRST + b * PAIRS + (unit + 1) * UP)
                    eng.dma_start(bass.AP(x1_dram.tensor, b * ((C * H + 2) * W) + W + unit * (U * W),
                                          [[H * W, C], [1, U * W]]),
                                  rows_out[0:C, :]).then_inc(x1_stored, 16)

                def begin_group(k, j):
                    group = k * GK + j
                    eng.wait_ge(xs_loaded[j % 2], (b * (NG // 2) + k * (GK // 2) + j // 2 + 1) * 16)
                    eng.wait_ge(par_taken, (b * G_TURNS + k) * 2 + (1 if j == 0 else 2))
                    for rows, scale, column in ((slice(0, 1), const_("inside", 128)[:, 0:1], NV),
                                                (slice(U + 1, U + 2), const_("inside", 128)[:, 1:2], NV + 1),
                                                (slice(1, U + 1), 1.0, TAPS)):
                        part = xs[j % 2][:, rows, 1:1 + W]
                        nc.scalar.activation(part, part, ACT.Identity, scale=scale,
                                             bias=par[:, j, column:column + 1]).then_inc(xs_centred, 1)
                    eng.wait_ge(xs_centred, (b * NG + group + 1) * 3)
                    if not lags_:
                        for i, t in enumerate(Y_PE):
                            nc.scalar.activation(diag[j % 2][:, i, :], const_("ident", 128), ACT.Identity,
                                                 scale=par[:, j, t:t + 1]).then_inc(diag_ready, 1)
                    eng.wait_ge(y_stored[j % 2], FIRST_STORE + (b * (NG // 2) + k * (GK // 2) + j // 2) * 16)
                    nc.scalar.activation(ys[j % 2], xs[j % 2][:, 0:U, 0:W], ACT.Identity, scale=par[:, j, 0:1],
                                         bias=par[:, j, TAPS + 1:NV]).then_inc(y_begun, 1)

                def rows(base, first, last):
                    for r in range(first, last):
                        high_half(base, r)

                if not rest:
                    rows(0, 0, A_ROWS)
                    rows_only(eng, high_half)
                    return
                attention(b, lambda first, last: rows(0, first, last))
                eng.wait_ge(v_ready, b * VP + 1)
                copy(vb[1][:, U, 1:1 + W], const_("zero", C)).then_inc(v_topped, 1)
                copy(vb[1][:, U + 1, 1:1 + W], x1_bank[1][0:C, 0:W]).then_inc(v_kept, 1)
                eng.wait_ge(v_topped, b + 1)
                v_rows(0, 0)
                rows(0, 14, 16)
                with eng.Fori(0, U_TURNS) as k:
                    for c in range(UK):
                        v_rows(k * UK + c + 1, c + 1)
                        r0, r1 = U_AT[c]
                        rows(T1_AT + k * U_ROWS, r0, r1 - 1)
                        x1_rows(k * UK + c, mom_turn, c * UP)
                        rows(T1_AT + k * U_ROWS, r1 - 1, r1)
                    copy(x1_mom[:, :, bass.ds(k * (UK * UP), UK * UP)], mom_turn[:, :, :]).then_inc(x1_summed, 1)
                v_rows(NU - 1, NU - 1)
                rows(D_AT, 0, 2)
                x1_rows(NU - 2, x1_mom, (NU - 2) * UP)
                rows(D_AT, 2, 6)
                x1_rows(NU - 1, x1_mom, (NU - 1) * UP)
                rows(D_AT, 6, 8)
                eng.wait_ge(dve_dyn, b * N_DD + at(DVE_DYN, "vareps1"))
                nc.scalar.activation(gm1[:, 4:5], gm1[:, 3:4], ACT.Sqrt).then_inc(act_dyn, 1)
                rows(D_AT, 8, 11)
                eng.wait_ge(pe_dyn, b * N_PD + at(PE_DYN, "hidden"))
                nc.scalar.activation(hid[:, :], bank[3][0:RED, 0:1], ACT.Sigmoid, bias=bn_sb[:, 1:2],
                                     scale=bn_sb[:, 0:1]).then_inc(act_dyn, 1)
                rows(D_AT, 11, 16)

                def groups(k, last=False):
                    for j in range(GK):
                        rows(T2_AT + k * G_ROWS, j * G_EACH, j * G_EACH + 3)
                        if j < GK - 1:
                            begin_group(k, j + 1)
                        elif not last:
                            begin_group(k + 1, 0)
                        rows(T2_AT + k * G_ROWS, j * G_EACH + 3, (j + 1) * G_EACH)

                begin_group(0, 0)
                with eng.Fori(0, G_TURNS - 1) as k:
                    groups(k)
                groups(G_TURNS - 1, last=True)

            def attention(b, rows):
                def pe(name):
                    eng.wait_ge(pe_att, b * N_PA + at(PE_ATT, name))

                def dve(name):
                    eng.wait_ge(dve_att, b * N_DA + at(DVE_ATT, name))

                def step(ins):
                    ins.then_inc(act_att, 1)

                eng.wait_ge(lags_summed, b + 1)
                eng.wait_ge(x1_stored, FIRST + b * NU * 16)
                for dx in (1, 2):
                    step(copy(lags[:, dx, :], acc[dx][0:K1, 0:LAG_W]))
                step(copy(edge_cols_kept[:, :, :], edge_cols[:, :, :]))
                eng.wait_ge(act_att, b * N_AA + at(ACT_ATT, "edges"))
                rows(0, 2)
                dve("vareps0")
                step(nc.scalar.activation(gm0[:, 4:5], gm0[:, 3:4], ACT.Sqrt))
                rows(2, 4)
                pe("folded_v")
                step(copy(v_foldT[:, :], bank[3][0:K1, 0:C]))
                step(copy(v_fold[:, :], bank[3][0:C, C:C + K1]))
                rows(4, 6)
                for stored in y_stored:
                    eng.wait_ge(stored, FIRST_STORE + b * (NG // 2) * 16)
                for j in range(7):
                    pe(f"lag_w{j}")
                    n = min(2, NL - 2 * j)
                    step(copy(lagw[:, 2 * j:2 * j + n, :].rearrange("p d a -> p (d a)"), bank[2 + j % 2][0:K1, 0:n * QK]))
                rows(6, 9)
                for j, (side, _) in enumerate(EDGES):
                    n = EP if side < 2 else 128
                    if j == 5:
                        rows(9, 10)
                    pe(f"ring{j}")
                    step(copy(ring_sb[0:n, j % 2, :], bank[2 + j % 2][0:n, 0:QK]))
                rows(10, 11)
                dve("norm_sq")
                step(nc.scalar.activation(nrm[:, 4:6], nrm[:, 2:4], ACT.Sqrt))
                rows(11, 12)
                dve("max_neg")
                step(nc.scalar.activation(att[:, 3, :], att[:, 2, :], ACT.Exp, bias=nrm[:, 0:1],
                                          accum_out=nrm[:, 1:2]))
                rows(12, 14)

            pipeline(eng, step)


def kernel(x, L0_conv_qkv_w, L0_conv_qkv_dw_w, L0_conv_proj_w, L1_conv_w1, L1_conv_gamma, L1_conv_beta,
           L1_conv_running_mean, L1_conv_running_var, L1_conv_w2, L1_conv_b2, L1_conv_bias):
    import concourse.bacc as bacc
    from concourse.bass_utils import run_bass_kernel_spmd

    dw = np.asarray(L0_conv_qkv_dw_w).reshape(3 * C, TAPS)
    dw_t = dw[0:QK].T
    lag_t = np.zeros((TAPS, NL, QK), np.float32)
    for d, (dx, dy) in enumerate(LAGS):
        for t in range(TAPS):
            ty, tx = t // 3 + dy, t % 3 + dx
            if 0 <= ty < 3 and 0 <= tx < 3:
                lag_t[t, d] = dw_t[ty * 3 + tx]
    arrays = {
        "x": np.asarray(x),
        "qkv_wT": np.asarray(L0_conv_qkv_w)[:, :, 0, 0].T,
        "dw_t": dw_t,
        "lag_t": lag_t,
        "dw_rep": np.broadcast_to(dw_t, (K1, TAPS, QK)),
        "dw_v": dw[QK:],
        "proj_wT": np.asarray(L0_conv_proj_w)[:, :, 0, 0].T,
        "w1T": np.asarray(L1_conv_w1).T,
        "bn": np.stack([np.asarray(a) for a in (L1_conv_gamma, L1_conv_beta, L1_conv_running_mean,
                                                L1_conv_running_var)], 1),
        "w2T": np.asarray(L1_conv_w2).reshape(C, TAPS, RED).transpose(2, 1, 0),
        "b2": np.asarray(L1_conv_b2).reshape(C, TAPS),
        "bias": np.asarray(L1_conv_bias).reshape(C, 1),
        "const": constants(),
        "ends": np.concatenate([np.ones((1, W), np.float32), np.zeros((K1, W), np.float32)]),
    }
    arrays = {f"in_{name}": np.ascontiguousarray(a) for name, a in arrays.items()}
    nc = bacc.Bacc("TRN2", target_bir_lowering=False, num_devices=1)
    args = [nc.dram_tensor(name, a.shape, mybir.dt.from_np(a.dtype), kind="ExternalInput").ap()
            for name, a in arrays.items()]
    out = nc.dram_tensor("out", (B, C, H, W), mybir.dt.float32, kind="ExternalOutput").ap()
    build(nc, *args, out)
    result = run_bass_kernel_spmd(nc, [arrays], core_ids=[0])
    return result.results[0]["out"]
```
